# Optimizing a Trainium2 kernel written in Bass

```python
import numpy as np
import jax
import jax.numpy as jnp

def _softmax(x, axis=-1):
    return jax.nn.softmax(x, axis=axis)

def _gelu(x):
    return jax.nn.gelu(x, approximate=True)

def _silu(x):
    return jax.nn.silu(x)

def _sigmoid(x):
    return jax.nn.sigmoid(x)

def _layernorm(x, axis=-1, eps=1e-05):
    m = jnp.mean(x, axis=axis, keepdims=True)
    v = jnp.var(x, axis=axis, keepdims=True)
    return (x - m) / jnp.sqrt(v + eps)

def _scatter_add(tgt, idx, src, axis=0):
    return tgt.at[idx].add(src)

def _segment_sum(src, seg, n):
    return jax.ops.segment_sum(src, seg, n)
kernel_name = 'mk_adj_preln_d2_adj_r2_135344'

def setup_inputs(seed: int=0):
    np.random.seed(seed)
    _w = jnp.asarray

    def _rec_inputs():
        import jax
        import jax.numpy as jnp
        _gk = jax.random.key(seed)
        x = -0.0005207 + 1.001 * jax.random.normal(jax.random.fold_in(_gk, 1), (128, 64, 256), jnp.float32)
        _a = jax.random.bernoulli(jax.random.fold_in(_gk, 2), 0.0625, (128, 64, 64))
        _a = jnp.logical_or(_a, jnp.swapaxes(_a, -1, -2))
        _a = jnp.logical_or(_a, jnp.eye(64, dtype=bool))
        adj = _a.astype(jnp.int32)
        return (x, adj)
    x, adj = _rec_inputs()

    def _L0_gnn_setup():
        import jax, jax.numpy as jnp
        import numpy as np
        NEG_INF = -1e+30
        NEG_SLOPE = 0.2
        key = jax.random.key(seed)
        k1, k2, k3, k4, k5 = jax.random.split(key, 5)
        B, N, D, H = (2, 1024, 256, 8)
        k = D // H
        return {'x': jax.random.normal(k1, (B, N, D), dtype=jnp.float32), 'A': jax.random.randint(k2, (B, N, N), 0, 2, dtype=jnp.int32), 'W_proj': jax.random.normal(k3, (D, D), dtype=jnp.float32) * (1.0 / np.sqrt(D)), 'W_att': jax.random.normal(k4, (H, 2 * k), dtype=jnp.float32) * (1.0 / np.sqrt(2 * k)), 'b_att': jax.random.normal(k5, (H,), dtype=jnp.float32) * 0.01}
    _L0_gnn_all = _L0_gnn_setup()
    _L0_gnn_in = {k: v for k, v in _L0_gnn_all.items() if k in ('W_proj', 'W_att', 'b_att')}
    del _L0_gnn_all

    def _L1_gnn_setup():
        import jax, jax.numpy as jnp
        import numpy as np
        L = 3
        D = 256
        B, N = (8, 512)
        EPS = 1e-05

        def layernorm(x, gamma, beta):
            mu = jnp.mean(x, axis=-1, keepdims=True)
            var = jnp.var(x, axis=-1, keepdims=True)
            return (x - mu) * jax.lax.rsqrt(var + EPS) * gamma + beta
        key = jax.random.key(seed)
        ks = jax.random.split(key, 12)
        s = 1.0 / np.sqrt(D)
        node_features = jax.random.normal(ks[0], (B, N, D), dtype=jnp.float32)
        adjacency_matrix = jax.random.randint(ks[1], (B, N, N), 0, 2, dtype=jnp.int32)
        return {'node_features': node_features, 'adjacency_matrix': adjacency_matrix, 'attn_w': jax.random.normal(ks[2], (L, 2 * D), dtype=jnp.float32) * (1.0 / np.sqrt(2 * D)), 'attn_b': jax.random.normal(ks[3], (L,), dtype=jnp.float32) * 0.01, 'W1': jax.random.normal(ks[4], (L, D, 4 * D), dtype=jnp.float32) * s, 'b1': jnp.zeros((L, 4 * D), dtype=jnp.float32), 'W2': jax.random.normal(ks[5], (L, 4 * D, D), dtype=jnp.float32) * (1.0 / np.sqrt(4 * D)), 'b2': jnp.zeros((L, D), dtype=jnp.float32), 'g1': jnp.ones((L, D), dtype=jnp.float32), 'beta1': jnp.zeros((L, D), dtype=jnp.float32), 'g2': jnp.ones((L, D), dtype=jnp.float32), 'beta2': jnp.zeros((L, D), dtype=jnp.float32)}
    _L1_gnn_all = _L1_gnn_setup()
    _L1_gnn_in = {k: v for k, v in _L1_gnn_all.items() if k in ('attn_w', 'attn_b', 'W1', 'b1', 'W2', 'b2', 'g1', 'beta1', 'g2', 'beta2')}
    del _L1_gnn_all
    return {'x': x, 'adj': adj, 'L0_gnn_W_proj': _L0_gnn_in['W_proj'], 'L0_gnn_W_att': _L0_gnn_in['W_att'], 'L0_gnn_b_att': _L0_gnn_in['b_att'], 'L1_gnn_attn_w': _L1_gnn_in['attn_w'], 'L1_gnn_attn_b': _L1_gnn_in['attn_b'], 'L1_gnn_W1': _L1_gnn_in['W1'], 'L1_gnn_b1': _L1_gnn_in['b1'], 'L1_gnn_W2': _L1_gnn_in['W2'], 'L1_gnn_b2': _L1_gnn_in['b2'], 'L1_gnn_g1': _L1_gnn_in['g1'], 'L1_gnn_beta1': _L1_gnn_in['beta1'], 'L1_gnn_g2': _L1_gnn_in['g2'], 'L1_gnn_beta2': _L1_gnn_in['beta2']}

def reference(x, adj, L0_gnn_W_proj, L0_gnn_W_att, L0_gnn_b_att, L1_gnn_attn_w, L1_gnn_attn_b, L1_gnn_W1, L1_gnn_b1, L1_gnn_W2, L1_gnn_b2, L1_gnn_g1, L1_gnn_beta1, L1_gnn_g2, L1_gnn_beta2):
    import jax
    import jax.numpy as jnp

    def _L0_gnn_ref(x, A, W_proj, W_att, b_att):
        import jax, jax.numpy as jnp
        import numpy as np
        NEG_INF = -1e+30
        NEG_SLOPE = 0.2
        B, N, _ = x.shape
        H, two_k = W_att.shape
        k = two_k // 2
        xp = jnp.einsum('bnd,do->bno', x, W_proj)
        xh = xp.reshape(B, N, H, k).transpose(0, 2, 1, 3)
        a_src = jnp.einsum('bhnk,hk->bhn', xh, W_att[:, :k])
        a_dst = jnp.einsum('bhnk,hk->bhn', xh, W_att[:, k:])
        scores = a_src[:, :, :, None] + a_dst[:, :, None, :] + b_att[None, :, None, None]
        scores = jax.nn.leaky_relu(scores, negative_slope=NEG_SLOPE)
        mask = (A > 0)[:, None, :, :]
        scores = jnp.where(mask, scores, NEG_INF)
        att = jax.nn.softmax(scores, axis=-1)
        out = jax.nn.relu(jnp.einsum('bhij,bhjk->bhik', att, xh))
        return out.transpose(0, 2, 1, 3).reshape(B, N, H * k)

    def _L1_gnn_ref(node_features, adjacency_matrix, attn_w, attn_b, W1, b1, W2, b2, g1, beta1, g2, beta2):
        import jax, jax.numpy as jnp
        import numpy as np
        L = 3
        D = 256
        B, N = (8, 512)
        EPS = 1e-05

        def layernorm(x, gamma, beta):
            mu = jnp.mean(x, axis=-1, keepdims=True)
            var = jnp.var(x, axis=-1, keepdims=True)
            return (x - mu) * jax.lax.rsqrt(var + EPS) * gamma + beta
        n = adjacency_matrix.shape[-1]
        mask = adjacency_matrix.astype(jnp.float32) + jnp.eye(n, dtype=jnp.float32) > 0
        x = node_features
        d = x.shape[-1]
        for l in range(attn_w.shape[0]):
            si = x @ attn_w[l, :d]
            sj = x @ attn_w[l, d:]
            scores = si[:, :, None] + sj[:, None, :] + attn_b[l]
            scores = jnp.where(scores >= 0, scores, 0.2 * scores)
            scores = jnp.where(mask, scores, -jnp.inf)
            attn = jax.nn.softmax(scores, axis=-1)
            agg = jnp.einsum('bij,bjd->bid', attn, x)
            h = layernorm(x + agg, g1[l], beta1[l])
            ff = jax.nn.gelu(h @ W1[l] + b1[l], approximate=False) @ W2[l] + b2[l]
            x = layernorm(h + ff, g2[l], beta2[l])
        return x
    h = jnp.maximum(_layernorm(x, axis=-1), 0.0)
    x = x + _L0_gnn_ref(h, adj, L0_gnn_W_proj, L0_gnn_W_att, L0_gnn_b_att)
    h = jnp.maximum(_layernorm(x, axis=-1), 0.0)
    x = x + _L1_gnn_ref(h, adj, L1_gnn_attn_w, L1_gnn_attn_b, L1_gnn_W1, L1_gnn_b1, L1_gnn_W2, L1_gnn_b2, L1_gnn_g1, L1_gnn_beta1, L1_gnn_g2, L1_gnn_beta2)
    return x

_drawn_inputs = setup_inputs


def setup_inputs(seed=0):
    import zlib

    import numpy as np

    out = dict(_drawn_inputs(seed))
    spreads = {'L1_gnn_b1': (0.0, 0.1),
     'L1_gnn_b2': (0.0, 0.1),
     'L1_gnn_g1': (1.0, 0.2),
     'L1_gnn_beta1': (0.0, 0.1),
     'L1_gnn_g2': (1.0, 0.2),
     'L1_gnn_beta2': (0.0, 0.1)}
    factors = {'L0_gnn_b_att': 64.0, 'L1_gnn_attn_b': 64.0}
    for name, (base, spread) in spreads.items():
        noise = np.random.default_rng([zlib.crc32(name.encode()), seed]).standard_normal(out[name].shape)
        drawn = base * np.exp(spread * noise) if base else spread * noise
        out[name] = jnp.asarray(drawn.astype(out[name].dtype))
    for name, factor in factors.items():
        out[name] = (out[name] * factor).astype(out[name].dtype)
    return out
```

```python
from contextlib import ExitStack

import concourse.bass as bass
from concourse import mybir

F32 = mybir.dt.float32
F32R = mybir.dt.float32r
I32 = mybir.dt.int32
ALU = mybir.AluOpType
ACT = mybir.ActivationFunctionType
AX = mybir.AxisListType.X

P = 128
NEG = -1e30
SLOPE = 0.2
EPS = 1e-5


def at_least(eng, sem, value):
    if not isinstance(value, int) or value > 0:
        eng.wait_ge(sem, value)


def pause(eng, sem, value, own):
    if not isinstance(value, int) or value > 0:
        eng.wait_ge(sem, value)
        eng.sem_inc(own, 1)


class Steps:

    def __init__(self, eng, sem, per):
        self.eng, self.sem, self.per, self.base, self.k = eng, sem, per, 0, 0

    def unit(self, n):
        assert self.k in (0, self.per), self.k
        self.base, self.k = n * self.per, 0

    def done(self, instruction):
        self.k += 1
        instruction.then_inc(self.sem, 1)

    def wait(self):
        self.eng.wait_ge(self.sem, self.base + self.k)


def graph_net(nc, x, adj, w_proj, w_att, b_att, attn_w, attn_b, w1, b1, w2, b2, g1, beta1, g2, beta2, out):
    B, N, D = x.shape
    H, K2 = w_att.shape
    HK = K2 // 2
    L, _, F = w1.shape
    NT = B * N // P
    GPT = P // N
    KD = D // P
    CF = F // P
    TG = 4
    NG = NT // TG
    TOK = TG * P
    QG = 4
    LAPS = NG // QG
    SLOTS = L * QG
    WC = D + 2 * H
    HC = HK + 1
    RING = 2

    x_v = x.rearrange("(t g) n d -> (g n) t d", g=GPT)
    out_v = out.rearrange("(t g) n d -> (g n) t d", g=GPT)
    adj_v = adj.rearrange("(t g) i j -> (g i) t j", g=GPT)
    res_d = nc.dram_tensor("first_block_out", (P, NT, D), F32, kind="Internal").ap()
    act_d = nc.dram_tensor("second_block_in", (P, NT, D), F32, kind="Internal").ap()

    def row(ap, n):
        return ap.rearrange("(a n) -> a n", a=1).broadcast_to([P, n])

    ctx = ExitStack()
    with ctx:
        def sb(name, shape, dt=F32, where=None):
            return (where or ctx).enter_context(nc.sbuf_tensor(name, shape, dt))

        def sem(name):
            return ctx.enter_context(nc.semaphore(name))

        bank = [ctx.enter_context(nc.psum_tensor(f"bank{i}", [P, 512], F32)) for i in range(8)]

        ident = sb("ident", [P, P])
        node_of = sb("node_of", [P, N])
        same_graph = sb("same_graph", [P, P])
        minus_half = sb("minus_half", [P, TG])
        w1_hi, w1_lo = (sb(n, [P, L, KD, F], F32R) for n in ("w1_hi", "w1_lo"))
        w2_hi, w2_lo = (sb(n, [P, L, CF, D], F32R) for n in ("w2_hi", "w2_lo"))
        b1_col = sb("b1_col", [P, L, CF])
        g1_row, c1_row, g2_row, beta2_row = (sb(n, [P, L, D]) for n in ("g1_row", "c1_row", "g2_row", "beta2_row"))
        att_row = sb("att_row", [P, L, 2, D])
        attb_row = sb("attb_row", [P, L])

        setup = ExitStack()
        projection = ctx.enter_context(ExitStack())
        wcat_hi, wcat_lo = (sb(n, [P, KD, WC], F32R, where=projection) for n in ("wcat_hi", "wcat_lo"))
        batt_row = sb("batt_row", [P, H], where=projection)
        with setup:
            stage = sb("stage", [P, 2, KD * F], where=setup)
            wcat = sb("wcat", [P, KD, WC], where=setup)
            watt_row = sb("watt_row", [P, 2, H, HK], where=setup)
            prod = sb("prod", [P, H, HK], where=setup)
            b1_raw = sb("b1_raw", [P, L, CF], where=setup)
            g1_col, beta1_col = (sb(n, [P, L, KD], where=setup) for n in ("g1_col", "beta1_col"))
            b2_row = sb("b2_row", [P, L, D], where=setup)
            s_w = [sem(f"stage_loaded{i}") for i in range(2)]
            s_col, s_rows, s_cat = sem("columns_loaded"), sem("rows_loaded"), sem("wcat_loaded")
            s_fill, s_const = sem("consts_filled"), sem("consts_made")
            s_bias, s_scaled = sem("bias_products"), sem("weights_scaled")
            s_hi, s_lo, s_su = sem("weight_hi"), sem("weight_lo"), sem("setup_vector")
            s_b1, s_same = sem("bias_kept"), sem("same_graph_made")
            JOBS = [(l, which) for l in range(L) for which in (1, 2)]
            blk = setup.enter_context(nc.Block())

            @blk.sync
            def _(sp):
                with nc.allow_non_contiguous_dma(reason="small columns"):
                    for k in range(KD):
                        sp.dma_start(wcat[:, k, 0:D], w_proj[k * P:(k + 1) * P, :]).then_inc(s_cat, 16)
                    for i in range(2):
                        sp.dma_start(watt_row[:, i], w_att[:, i * HK:(i + 1) * HK].rearrange("(a h) k -> a h k", a=1)
                                     .broadcast_to([P, H, HK])).then_inc(s_cat, 16)
                    sp.dma_start(b1_raw[:], b1.rearrange("l (c p) -> p l c", p=P)).then_inc(s_col, 16)
                    sp.dma_start(g1_col[:], g1.rearrange("l (c p) -> p l c", p=P)).then_inc(s_col, 16)
                    sp.dma_start(beta1_col[:], beta1.rearrange("l (c p) -> p l c", p=P)).then_inc(s_col, 16)
                    for n, (l, which) in enumerate(JOBS):
                        if n >= 2:
                            sp.wait_ge(s_lo, n - 1 + 1)
                        if which == 1:
                            sp.dma_start(stage[:, n % 2, :].rearrange("p (c f) -> p c f", c=KD),
                                         w1[l].rearrange("(c p) f -> p c f", p=P)).then_inc(s_w[n % 2], 16)
                        else:
                            sp.dma_start(stage[:, n % 2, :].rearrange("p (c d) -> p c d", c=CF),
                                         w2[l].rearrange("(c p) d -> p c d", p=P)).then_inc(s_w[n % 2], 16)

            @blk.gpsimd
            def _(pool):
                pool.memset(ident[:], 0.0).then_inc(s_fill, 1)
                pool.memset(node_of[:], 0.0).then_inc(s_fill, 1)
                pool.memset(minus_half[:], -0.5).then_inc(s_const, 1)
                pool.wait_ge(s_fill, 2)
                pool.affine_select(out=ident[:], in_=ident[:], compare_op=ALU.not_equal, fill=1.0, base=0,
                                   pattern=[[-1, P]], channel_multiplier=1).then_inc(s_const, 1)
                pool.affine_select(out=node_of[:], in_=node_of[:], compare_op=ALU.not_equal, fill=1.0, base=0,
                                   pattern=[[-1, N]], channel_multiplier=1).then_inc(s_fill, 1)
                pool.wait_ge(s_fill, 3)
                pool.affine_select(out=node_of[:], in_=node_of[:], compare_op=ALU.not_equal, fill=1.0, base=-N,
                                   pattern=[[-1, N]], channel_multiplier=1).then_inc(s_const, 1)
                with nc.allow_non_contiguous_dma(reason="broadcast rows"):
                    for l in range(L):
                        for dst, src in ((g1_row, g1), (c1_row, beta1), (g2_row, g2), (beta2_row, beta2), (b2_row, b2)):
                            pool.dma_start(dst[:, l, :], row(src[l], D)).then_inc(s_rows, 16)
                        pool.dma_start(att_row[:, l].rearrange("p a d -> p (a d)"), row(attn_w[l], 2 * D)).then_inc(s_rows, 16)
                    pool.dma_start(attb_row[:], row(attn_b, L)).then_inc(s_rows, 16)
                    pool.dma_start(batt_row[:], row(b_att, H)).then_inc(s_rows, 16)
                pool.wait_ge(s_rows, 16 * (6 * L + 2))
                pool.tensor_tensor(c1_row[:], c1_row[:], b2_row[:], ALU.add).then_inc(s_const, 1)

            @blk.tensor
            def _(pe):
                pe.wait_ge(s_col, 48)
                for l in range(L):
                    n = 2 * l
                    pe.wait_ge(s_w[0], 16 * (l + 1))
                    for c in range(CF):
                        for k in range(KD):
                            mm = pe.matmul(bank[0][:, l * CF + c:l * CF + c + 1],
                                           stage[:, n % 2, k * F + c * P:k * F + (c + 1) * P], beta1_col[:, l, k:k + 1],
                                           start=(k == 0), stop=(k == KD - 1))
                    mm.then_inc(s_bias, 1)

            @blk.scalar
            def _(act):
                act.wait_ge(s_su, 2 * KD * 2)
                act.copy(wcat_hi[:], wcat[:]).then_inc(s_hi, 1)
                for n, (l, which) in enumerate(JOBS):
                    if which == 1:
                        act.wait_ge(s_scaled, (l + 1) * KD)
                        act.copy(w1_hi[:, l].rearrange("p c f -> p (c f)"), stage[:, n % 2, :]).then_inc(s_hi, 1)
                    else:
                        act.wait_ge(s_w[1], 16 * (l + 1))
                        act.copy(w2_hi[:, l].rearrange("p c f -> p (c f)"), stage[:, n % 2, :]).then_inc(s_hi, 1)

            @blk.vector
            def _(dve):
                dve.memset(same_graph[:], 0.0).then_inc(s_same, 1)
                dve.wait_ge(s_same, 1)
                for g in range(GPT):
                    dve.memset(same_graph[g * N:(g + 1) * N, g * N:(g + 1) * N], 1.0).then_inc(s_same, 1)
                dve.wait_ge(s_cat, 16 * (KD + 2))
                done = 0
                for k in range(KD):
                    for i in range(2):
                        if done:
                            dve.wait_ge(s_su, done)
                        dve.tensor_tensor(prod[:], wcat[:, k, 0:D].rearrange("p (h k) -> p h k", h=H), watt_row[:, i],
                                          ALU.mult).then_inc(s_su, 1)
                        dve.wait_ge(s_su, done + 1)
                        dve.tensor_reduce(wcat[:, k, D + i * H:D + (i + 1) * H], prod[:], AX, ALU.add).then_inc(s_su, 1)
                        done += 2
                dve.wait_ge(s_hi, 1)
                dve.tensor_tensor(wcat_lo[:], wcat[:], wcat_hi[:].bitcast(F32), ALU.subtract).then_inc(s_lo, 1)
                dve.wait_ge(s_col, 48)
                for n, (l, which) in enumerate(JOBS):
                    if which == 1:
                        dve.wait_ge(s_bias, l + 1)
                        dve.tensor_tensor(b1_col[:, l], bank[0][:, l * CF:(l + 1) * CF], b1_raw[:, l], ALU.add).then_inc(s_b1, 1)
                        for k in range(KD):
                            w = stage[:, n % 2, k * F:(k + 1) * F]
                            dve.tensor_scalar(w, w, g1_col[:, l, k:k + 1], None, ALU.mult).then_inc(s_scaled, 1)
                        dve.wait_ge(s_scaled, (l + 1) * KD)
                        hi, lo = w1_hi, w1_lo
                    else:
                        hi, lo = w2_hi, w2_lo
                    dve.wait_ge(s_hi, n + 2)
                    dve.tensor_tensor(lo[:, l].rearrange("p c f -> p (c f)"), stage[:, n % 2, :],
                                      hi[:, l].rearrange("p c f -> p (c f)").bitcast(F32), ALU.subtract).then_inc(s_lo, 1)
                dve.wait_ge(s_lo, len(JOBS) + 1)

        first = ExitStack()
        with first:
            XR = 16
            xin = sb("xin", [P, XR, D], where=first)
            adjin = sb("adjin", [P, XR, N], I32, where=first)
            hrelu = sb("hrelu", [P, 2, D], where=first)
            hT_hi, hT_lo = (sb(n, [P, 2, D], F32R, where=first) for n in ("hT_hi", "hT_lo"))
            xh = sb("xh", [P, 4, H, HC], where=first)
            a_src = sb("a_src", [P, 2, H], where=first)
            a_dst = sb("a_dst", [P, 2, H], where=first)
            dst_diag = sb("dst_diag", [P, H, N], where=first)
            no_edge = sb("no_edge", [P, N], where=first)
            masked, scored, leaky, shifted = (sb(n, [P, H, N], where=first) for n in ("masked", "scored", "leaky", "shifted"))
            top, top_s, top_l = (sb(n, [P, H], where=first) for n in ("top", "top_s", "top_l"))
            weights = sb("weights", [P, H, P], where=first)
            weights_T = sb("weights_T", [P, 2, H, P], where=first)
            inv = sb("inv", [P, H], where=first)
            headout = sb("headout", [P, D], where=first)
            x_res = sb("x_res", [P, 8, D], where=first)
            x_act = sb("x_act", [P, 8, D], where=first)
            stats = sb("stats", [P, 2, 6], where=first)
            mv = sb("mv", [P, 4, 2], where=first)
            rstd = sb("rstd", [P, 4, 1], where=first)
            nmr = sb("nmr", [P, 4, 1], where=first)
            mv2, rstd2, nmr2 = (sb(n, [P, 4, k], where=first) for n, k in (("mv2", 2), ("rstd2", 1), ("nmr2", 1)))
            vare, vare2 = (sb(n, [P, 4, 1], where=first) for n in ("vare", "vare2"))

            q_own, q_own_sp, q_ld, q_s, q_vs, q_vh = sem("q_paused"), sem("q_sync_paused"), sem("tiles_loaded"), sem("q_stats"), sem("q_score_steps"), sem("q_heads_steps")
            q_st = sem("first_stored")
            q_zero = sem("first_filled")
            q_mv, q_rs, q_nmr, q_h = sem("q_mean_var"), sem("q_rstd"), sem("q_shift"), sem("q_h")
            q_tr, q_hi, q_lo = sem("q_hT"), sem("q_hT_hi"), sem("q_hT_lo")
            q_xp, q_xh, q_asd, q_diag = sem("q_proj"), sem("q_xh"), sem("q_src_dst"), sem("q_diag")
            q_bc, q_msk, q_sc, q_d, q_e = sem("q_dst_spread"), sem("q_masked"), sem("q_scored"), sem("q_shifted"), sem("q_weights")
            q_wt, q_ev, q_ag = sem("q_weights_T"), sem("q_weights_T_kept"), sem("q_heads")
            q_res, q_mv2, q_rs2, q_nmr2, q_act = sem("q_res"), sem("q_mean_var2"), sem("q_rstd2"), sem("q_shift2"), sem("q_act")
            blk = first.enter_context(nc.Block())

            HEAD, LAG = 12, 7

            def steps(eng, step):
                for tau in range(HEAD):
                    step(tau, tau)
                with eng.Fori(HEAD // 4, NT // 4) as i:
                    for t in range(4):
                        step(i * 4 + t, t)
                for tau in range(NT, NT + LAG):
                    step(tau, tau)

            def has(T):
                return not isinstance(T, int) or 0 <= T < NT

            @blk.sync
            def _(sp):
                def load_group(g, part):
                    pause(sp, q_ld, 32 * g, q_own_sp)
                    sp.dma_start(xin[:, part * 4:part * 4 + 4, :], x_v[:, bass.ts(g, 4), :]).then_inc(q_ld, 16)
                    sp.dma_start(adjin[:, part * 4:part * 4 + 4, :], adj_v[:, bass.ts(g, 4), :]).then_inc(q_ld, 16)

                def store_group(g, half):
                    pause(sp, q_res, 4 * g + 4, q_own_sp)
                    pause(sp, q_act, 4 * g + 4, q_own_sp)
                    pause(sp, q_st, 32 * g, q_own_sp)
                    sp.dma_start(res_d[:, bass.ts(g, 4), :], x_res[:, half * 4:half * 4 + 4, :]).then_inc(q_st, 16)
                    sp.dma_start(act_d[:, bass.ts(g, 4), :], x_act[:, half * 4:half * 4 + 4, :]).then_inc(q_st, 16)

                for g in range(4):
                    load_group(g, g)
                with sp.Fori(0, NG // 4 - 1) as i:
                    for part in range(4):
                        store_group(i * 4 + part, part % 2)
                        load_group(i * 4 + (part + 4), part)
                for g in range(NG - 4, NG):
                    store_group(g, g % 2)
                sp.wait_ge(q_st, 32 * NG)

            @blk.tensor
            def _(pe):
                def step(tau, t):
                    T, r = tau - 6, (t - 6)
                    if has(T):
                        pe.wait_ge(q_ev, 2 * T + 2)
                        pe.wait_ge(q_xh, T + 1)
                        at_least(pe, q_res, T)
                        for h in range(H):
                            mm = pe.matmul(bank[7][:, h * HC:(h + 1) * HC], weights_T[:, r % 2, h, :],
                                           xh[:, r % 4, h, :], start=True, stop=True)
                        mm.then_inc(q_ag, 1)
                    T, r = tau - 5, (t - 5)
                    if has(T):
                        pe.wait_ge(q_e, 2 * T + 2)
                        at_least(pe, q_ev, 2 * T)
                        for h in range(H):
                            mm = pe.transpose(bank[5 + h // 4][:, (h % 4) * P:(h % 4 + 1) * P], weights[:, h, :], ident[:])
                        mm.then_inc(q_wt, 1)
                    T, r = tau - 4, (t - 4)
                    if has(T):
                        pe.wait_ge(q_diag, T + 1)
                        at_least(pe, q_msk, T)
                        pe.matmul(bank[4][:], same_graph[:], dst_diag[:].rearrange("p h j -> p (h j)"),
                                  start=True, stop=True).then_inc(q_bc, 1)
                    T, r = tau - 3, (t - 3)
                    if has(T):
                        pe.wait_ge(q_lo, T + 1)
                        at_least(pe, q_xh, T - 1)
                        at_least(pe, q_asd, 2 * (T - 1))
                        for k in range(KD):
                            for p, (a, w) in enumerate(((hT_hi, wcat_hi), (hT_hi, wcat_lo), (hT_lo, wcat_hi))):
                                mm = pe.matmul(bank[2 + r % 2][:, 0:WC], a[:, r % 2, k * P:(k + 1) * P], w[:, k, :],
                                               start=(k == 0 and p == 0), stop=(k == KD - 1 and p == 2))
                        mm.then_inc(q_xp, 1)
                    T, r = tau - 2, (t - 2)
                    if has(T):
                        pe.wait_ge(q_h, T + 1)
                        at_least(pe, q_lo, T - 1)
                        for k in range(KD):
                            mm = pe.transpose(bank[r % 2][:, k * P:(k + 1) * P], hrelu[:, r % 2, k * P:(k + 1) * P], ident[:])
                        mm.then_inc(q_tr, 1)

                steps(pe, step)

            @blk.scalar
            def _(act):
                def step(tau, t):
                    T, r = tau - 7, (t - 7)
                    if has(T):
                        act.wait_ge(q_nmr2, T + 1)
                        if r % 4 == 0:
                            at_least(act, q_st, 8 * (T - 4))
                        act.activation(x_act[:, T % 8, :],
                                       x_res[:, T % 8, :], ACT.Relu,
                                       bias=nmr2[:, r % 4, :], scale=rstd2[:, r % 4, :]).then_inc(q_act, 1)
                    T, r = tau - 5, (t - 5)
                    if has(T):
                        act.wait_ge(q_wt, T + 1)
                        at_least(act, q_ag, T - 1)
                        for b in range(2):
                            act.copy(weights_T[:, r % 2, 4 * b:4 * b + 4, :].rearrange("p h i -> p (h i)"),
                                     bank[5 + b][:]).then_inc(q_ev, 1)
                    T, r = tau - 4, (t - 4)
                    if has(T):
                        act.wait_ge(q_d, T + 1)
                        at_least(act, q_wt, T)
                        if isinstance(T, int) and T == 0:
                            act.wait_ge(q_zero, 1)
                        for g in range(GPT):
                            act.activation(weights[g * N:(g + 1) * N, :, g * N:(g + 1) * N],
                                           shifted[g * N:(g + 1) * N], ACT.Exp).then_inc(q_e, 1)
                    T, r = tau - 3, (t - 3)
                    if has(T):
                        act.wait_ge(q_xp, T + 1)
                        at_least(act, q_ag, T - 3)
                        if isinstance(T, int) and T == 0:
                            act.wait_ge(q_zero, 2)
                        act.copy(xh[:, r % 4, :, 0:HK], bank[2 + r % 2][:, 0:D].rearrange("p (h k) -> p h k", h=H)).then_inc(q_xh, 1)
                    T, r = tau - 2, (t - 2)
                    if has(T):
                        act.wait_ge(q_tr, T + 1)
                        at_least(act, q_xp, T - 1)
                        act.copy(hT_hi[:, r % 2, :], bank[r % 2][:, 0:D]).then_inc(q_hi, 1)
                    T, r = tau - 1, (t - 1)
                    if has(T):
                        act.wait_ge(q_nmr, T + 1)
                        at_least(act, q_tr, T - 1)
                        act.activation(hrelu[:, r % 2, :], xin[:, T % XR, :], ACT.Relu,
                                       bias=nmr[:, r % 4, :], scale=rstd[:, r % 4, :]).then_inc(q_h, 1)

                steps(act, step)

            @blk.gpsimd
            def _(pool):
                def step(tau, t):
                    T, r = tau - 6, (t - 6)
                    if has(T):
                        pool.wait_ge(q_mv2, 2 * T + 2)
                        pool.tensor_tensor(rstd2[:, r % 4, :], vare2[:, r % 4, :], minus_half[:, 0:1], ALU.pow).then_inc(q_rs2, 1)
                    T, r = tau - 4, (t - 4)
                    if has(T):
                        pool.wait_ge(q_msk, T + 1)
                        at_least(pool, q_d, T)
                        pool.tensor_tensor(scored[:], masked[:], a_src[:, r % 2, :].unsqueeze(2).broadcast_to([P, H, N]),
                                           ALU.add).then_inc(q_sc, 1)
                    T, r = tau - 3, (t - 3)
                    if has(T):
                        pool.wait_ge(q_asd, 2 * T + 2)
                        at_least(pool, q_bc, T)
                        pool.tensor_tensor(dst_diag[:], node_of[:].unsqueeze(1).broadcast_to([P, H, N]),
                                           a_dst[:, r % 2, :].unsqueeze(2).broadcast_to([P, H, N]), ALU.mult).then_inc(q_diag, 1)
                    T, r = tau, t
                    if has(T):
                        pool.wait_ge(q_mv, 2 * T + 2)
                        pool.tensor_tensor(rstd[:, r % 4, :], vare[:, r % 4, :], minus_half[:, 0:1], ALU.pow).then_inc(q_rs, 1)

                steps(pool, step)

            @blk.vector
            def _(dve):
                dve.memset(weights[:], 0.0).then_inc(q_zero, 1)
                dve.memset(xh[:, :, :, HK:HC], 1.0).then_inc(q_zero, 1)
                score = Steps(dve, q_vs, 5)
                heads = Steps(dve, q_vh, 3)

                def step(tau, t):
                    T, r = tau - 7, (t - 7)
                    if has(T):
                        dve.wait_ge(q_rs2, T + 1)
                        dve.scalar_tensor_tensor(nmr2[:, r % 4, :], mv2[:, r % 4, 0:1], -1.0, rstd2[:, r % 4, :],
                                                 ALU.mult, ALU.mult).then_inc(q_nmr2, 1)
                    T, r = tau - 6, (t - 6)
                    if has(T):
                        heads.unit(T)
                        dve.wait_ge(q_ag, T + 1)
                        G = bank[7][:, 0:H * HC].rearrange("p (h k) -> p h k", h=H)
                        heads.done(dve.reciprocal(inv[:].unsqueeze(2), G[:, :, HK:HC]))
                        heads.wait()
                        heads.done(dve.scalar_tensor_tensor(headout[:].rearrange("p (h k) -> p h k", h=H), G[:, :, 0:HK],
                                                            0.0, inv[:].unsqueeze(2).broadcast_to([P, H, HK]),
                                                            ALU.max, ALU.mult))
                        heads.wait()
                        if r % 4 == 0:
                            at_least(dve, q_st, 8 * (T - 4))
                        xr = x_res[:, T % 8, :]
                        dve.tensor_tensor(xr, headout[:], xin[:, T % XR, :], ALU.add).then_inc(q_res, 1)
                        pause(dve, q_res, T + 1, q_own)
                        heads.done(dve.bn_stats(stats[:, 1, :], xr))
                        heads.wait()
                        dve.sem_inc(q_own, 1)
                        dve.bn_aggr(mv2[:, r % 4, :], stats[:, 1, :]).then_inc(q_mv2, 1)
                        dve.wait_ge(q_mv2, 2 * T + 1)
                        dve.tensor_scalar(vare2[:, r % 4, :], mv2[:, r % 4, 1:2], EPS, None, ALU.add).then_inc(q_mv2, 1)
                    T, r = tau - 4, (t - 4)
                    if has(T):
                        score.unit(T)
                        score.done(dve.tensor_scalar(no_edge[:], adjin[:, T % XR, :], 0.0, NEG, ALU.is_le, ALU.mult))
                        score.wait()
                        dve.wait_ge(q_bc, T + 1)
                        at_least(dve, q_sc, T)
                        dve.tensor_tensor(masked[:], bank[4][:].rearrange("p (h j) -> p h j", h=H),
                                          no_edge[:].unsqueeze(1).broadcast_to([P, H, N]), ALU.add).then_inc(q_msk, 1)
                        dve.wait_ge(q_msk, T + 1)
                        score.done(dve.tensor_reduce(top[:], masked[:], AX, ALU.max))
                        score.wait()
                        score.done(dve.tensor_tensor(top_s[:], top[:], a_src[:, r % 2, :], ALU.add))
                        score.wait()
                        score.done(dve.scalar_tensor_tensor(top_l[:], top_s[:], SLOPE, top_s[:], ALU.mult, ALU.max))
                        dve.wait_ge(q_sc, T + 1)
                        score.done(dve.scalar_tensor_tensor(leaky[:], scored[:], SLOPE, scored[:], ALU.mult, ALU.max))
                        score.wait()
                        at_least(dve, q_e, 2 * T)
                        dve.tensor_tensor(shifted[:], leaky[:], top_l[:].unsqueeze(2).broadcast_to([P, H, N]),
                                          ALU.subtract).then_inc(q_d, 1)
                    T, r = tau - 3, (t - 3)
                    if has(T):
                        dve.wait_ge(q_xh, T + 1)
                        at_least(dve, q_sc, T - 1)
                        at_least(dve, q_diag, T - 1)
                        X = bank[2 + r % 2]
                        dve.tensor_tensor(a_src[:, r % 2, :], X[:, D:D + H], batt_row[:], ALU.add).then_inc(q_asd, 1)
                        dve.tensor_copy(a_dst[:, r % 2, :], X[:, D + H:D + 2 * H]).then_inc(q_asd, 1)
                    T, r = tau - 2, (t - 2)
                    if has(T):
                        dve.wait_ge(q_hi, T + 1)
                        at_least(dve, q_xp, T - 1)
                        dve.tensor_tensor(hT_lo[:, r % 2, :], bank[r % 2][:, 0:D], hT_hi[:, r % 2, :].bitcast(F32),
                                          ALU.subtract).then_inc(q_lo, 1)
                    T, r = tau - 1, (t - 1)
                    if has(T):
                        dve.wait_ge(q_rs, T + 1)
                        dve.scalar_tensor_tensor(nmr[:, r % 4, :], mv[:, r % 4, 0:1], -1.0, rstd[:, r % 4, :],
                                                 ALU.mult, ALU.mult).then_inc(q_nmr, 1)
                    T, r = tau, t
                    if has(T):
                        if t % 4 == 0:
                            pause(dve, q_ld, 32 * (T // 4 + 1), q_own)
                        dve.bn_stats(stats[:, 0, :], xin[:, T % XR, :]).then_inc(q_s, 1)
                        pause(dve, q_s, T + 1, q_own)
                        dve.bn_aggr(mv[:, r % 4, :], stats[:, 0, :]).then_inc(q_mv, 1)
                        dve.wait_ge(q_mv, 2 * T + 1)
                        dve.tensor_scalar(vare[:, r % 4, :], mv[:, r % 4, 1:2], EPS, None, ALU.add).then_inc(q_mv, 1)

                steps(dve, step)
        projection.close()
        second = ExitStack()
        with second:
            x_cur = sb("x_cur", [P, QG, TG, D], where=second)
            x_fin = sb("x_fin", [P, 2, TG, D], where=second)
            adj_raw = sb("adj_raw", [P, QG, TG, N], I32, where=second)
            mask = sb("mask", [P, QG, TG, N], where=second)
            mask_sum = sb("mask_sum", [P, TG, N], where=second)
            dots = sb("dots", [P, D], where=second)
            s_src, s_dst = (sb(n, [P, TG], where=second) for n in ("s_src", "s_dst"))
            src_b = sb("src_b", [P, TG], where=second)
            diag2 = sb("diag2", [P, TG, N], where=second)
            masked2, scored2, leaky2, shifted2 = (sb(n, [P, TG, N], where=second)
                                                  for n in ("masked2", "scored2", "leaky2", "shifted2"))
            top2, top2_s, top2_l = (sb(n, [P, TG], where=second) for n in ("top2", "top2_s", "top2_l"))
            attn = sb("attn", [P, TG, P], where=second)
            attn_T = sb("attn_T", [P, TG, P], where=second)
            row_sum, row_inv = (sb(n, [P, TG], where=second) for n in ("row_sum", "row_inv"))
            n_tok = sb("n_tok", [P, TG, D], where=second)
            nT_hi, nT_lo = (sb(n, [P, 2, KD, TOK], F32R, where=second) for n in ("nT_hi", "nT_lo"))
            base = sb("base", [P, 2, TG, D], where=second)
            hid = sb("hid", [P, RING, TOK], where=second)
            hid_hi, hid_lo = (sb(n, [P, RING, TOK], F32R, where=second) for n in ("hid_hi", "hid_lo"))
            y_tok = sb("y_tok", [P, TG, D], where=second)
            st_a, st_f = (sb(n, [P, TG, 6], where=second) for n in ("st_a", "st_f"))
            mv_a, mv_f = (sb(n, [P, TG, 2], where=second) for n in ("mv_a", "mv_f"))
            ve_a, ve_f, rs_a, rs_f, nm_a, nm_f = (sb(n, [P, TG], where=second)
                                                  for n in ("ve_a", "ve_f", "rs_a", "rs_f", "nm_a", "nm_f"))

            HID, FF = (bank[0], bank[1]), (bank[2], bank[3])
            SPREAD, ATT_T, AGG, NT_B = bank[4], bank[5], (bank[6], bank[7]), (bank[4], bank[5])

            s_in = [sem(f"group_loaded{g}") for g in range(QG)]
            s_res = [sem(f"res_loaded{i}") for i in range(2)]
            s_out = [sem(f"group_stored{i}") for i in range(2)]
            s_own, s_own_sp, s_zero, s_scd = sem("vector_paused"), sem("sync_paused"), sem("attn_zeroed"), sem("scores_leaky")
            s_hid, s_gelu, s_split, s_ff = sem("hidden"), sem("gelu"), sem("hidden_split"), sem("ff_chunk")
            s_y = sem("ff_read")
            s_stf, s_mvf, s_rsf, s_nmf, s_yn = sem("y_stats"), sem("y_mean_var"), sem("y_rstd"), sem("y_shift"), sem("y_norm")
            s_x, s_fin = sem("x_new"), sem("out_ready")
            s_dots, s_dg = sem("dots_done"), sem("dst_diagonal")
            s_spread, s_sc, s_sh, s_at = sem("dst_spread"), sem("score_steps"), sem("shifted_ready"), sem("attn_ready")
            s_atT, s_atk, s_agg = sem("attn_T_ready"), sem("attn_T_kept"), sem("aggregated")
            s_inv, s_u, s_sta, s_mva = sem("row_sums"), sem("residual_a"), sem("a_stats"), sem("a_mean_var")
            s_rsa, s_nma, s_n = sem("a_rstd"), sem("a_shift"), sem("n_ready")
            s_nT, s_nhi, s_nlo, s_base = sem("nT"), sem("nT_hi_ready"), sem("nT_lo_ready"), sem("base_ready")
            blk = second.enter_context(nc.Block())

            def laps(eng, before, lap):
                before()
                with eng.Fori(0, LAPS - 1) as i:
                    lap(i, False)
                lap(LAPS - 1, True)

            def layer_group(s):
                return s % SLOTS // QG, s % QG

            @blk.sync
            def _(sp):
                def load(lap, g):
                    n = lap * QG + g
                    sp.dma_start(x_cur[:, g], act_d[:, bass.ts(n, TG), :]).then_inc(s_in[g], 16)
                    sp.dma_start(adj_raw[:, g], adj_v[:, bass.ts(n, TG), :]).then_inc(s_in[g], 16)

                def load_res(lap, g):
                    n = lap * QG + g
                    sp.dma_start(x_fin[:, g % 2], res_d[:, bass.ts(n, TG), :]).then_inc(s_res[g % 2], 16)

                def before():
                    for g in range(QG):
                        load(0, g)
                    for g in range(2):
                        load_res(0, g)

                def lap(i, last):
                    for g in range(QG):
                        n = i * QG + g
                        pause(sp, s_fin, n + 1, s_own_sp)
                        sp.dma_start(out_v[:, bass.ts(n, TG), :], x_fin[:, g % 2]).then_inc(s_out[g % 2], 16)
                        if not last:
                            load(i + 1, g)
                        pause(sp, s_out[g % 2], 16 * (i * (QG // 2) + g // 2 + 1), s_own_sp)
                        if g < 2:
                            load_res(i, g + 2)
                        elif not last:
                            load_res(i + 1, g - 2)

                laps(sp, before, lap)

            @blk.tensor
            def _(pe):
                pe.sem_inc(s_ff, RING)

                def spread(V, s):
                    pe.wait_ge(s_dg, V + 1)
                    at_least(pe, s_nlo, 2 * V)
                    pe.matmul(SPREAD[:, 0:TG * N], same_graph[:], diag2[:].rearrange("p t j -> p (t j)"),
                              start=True, stop=True).then_inc(s_spread, 1)

                def turn_attn(V, s):
                    pe.wait_ge(s_at, GPT * (V + 1))
                    for t in range(TG):
                        mm = pe.transpose(ATT_T[:, t * P:(t + 1) * P], attn[:, t, :], ident[:])
                    mm.then_inc(s_atT, 1)

                def aggregate(V, s):
                    l, g = layer_group(s)
                    pe.wait_ge(s_atk, V + 1)
                    for t in range(TG):
                        mm = pe.matmul(AGG[t // 2][:, (t % 2) * D:(t % 2 + 1) * D], attn_T[:, t, :], x_cur[:, g, t, :],
                                       start=True, stop=True)
                    mm.then_inc(s_agg, 1)

                def turn_n(V, s):
                    for k in range(KD):
                        if k == 0:
                            pe.wait_ge(s_n, TG * (V + 1))
                        for t in range(TG):
                            mm = pe.transpose(NT_B[k][:, t * P:(t + 1) * P], n_tok[:, t, k * P:(k + 1) * P], ident[:])
                        mm.then_inc(s_nT, 1)

                def hidden(U, s, c):
                    l, g = layer_group(s)
                    if c == 0:
                        pe.wait_ge(s_nlo, KD * (U + 1))
                    pe.wait_ge(s_gelu, CF * U + c + 1)
                    for k in range(KD):
                        for p, (w, a) in enumerate(((w1_hi, nT_hi), (w1_hi, nT_lo), (w1_lo, nT_hi))):
                            mm = pe.matmul(HID[c % 2][:], w[:, l, k, c * P:(c + 1) * P], a[:, s % 2, k, :],
                                           start=(k == 0 and p == 0), stop=(k == KD - 1 and p == 2))
                    mm.then_inc(s_hid, 1)

                def output(U, s, c):
                    l, g = layer_group(s)
                    pe.wait_ge(s_split, CF * U + c + 1)
                    if c == 0:
                        pe.wait_ge(s_y, TG * U + TG)
                    for t in range(TG):
                        for p, (a, w) in enumerate(((hid_hi, w2_hi), (hid_hi, w2_lo), (hid_lo, w2_hi))):
                            mm = pe.matmul(FF[t // 2][:, (t % 2) * D:(t % 2 + 1) * D], a[:, c % RING, t * P:(t + 1) * P],
                                           w[:, l, c, :], start=(c == 0 and t % 2 == 0 and p == 0),
                                           stop=(c == CF - 1 and p == 2), skip_group_check=True)
                    mm.then_inc(s_ff, 1)

                def before():
                    spread(0, 0)
                    turn_attn(0, 0)
                    aggregate(0, 0)
                    turn_n(0, 0)

                def lap(i, last):
                    for s in range(SLOTS):
                        U, nxt = i * SLOTS + s, not (last and s == SLOTS - 1)
                        V = U + 1
                        for c in range(CF):
                            hidden(U, s, c)
                            if nxt and c == 3:
                                spread(V, s + 1)
                            if nxt and c == 5:
                                turn_attn(V, s + 1)
                            if c >= 2:
                                output(U, s, c - 2)
                            if nxt and c == 5:
                                aggregate(V, s + 1)
                        if nxt:
                            turn_n(V, s + 1)
                        output(U, s, CF - 2)
                        output(U, s, CF - 1)

                laps(pe, before, lap)

            @blk.scalar
            def _(act):
                act.sem_inc(s_gelu, 2)

                def gelu(U, s, c):
                    l, g = layer_group(s)
                    act.wait_ge(s_hid, CF * U + c + 1)
                    act.wait_ge(s_ff, CF * U + c + 1)
                    act.activation(hid[:, c % RING, :], HID[c % 2][:], ACT.Gelu, bias=b1_col[:, l, c:c + 1])
                    act.activation(hid_hi[:, c % RING, :], HID[c % 2][:], ACT.Gelu, bias=b1_col[:, l, c:c + 1]).then_inc(s_gelu, 1)

                def norm_y(U, ts):
                    for t in ts:
                        act.wait_ge(s_nmf, U + 1)
                        act.activation(y_tok[:, t, :], y_tok[:, t, :], ACT.Identity, bias=nm_f[:, t:t + 1],
                                       scale=rs_f[:, t:t + 1]).then_inc(s_yn, 1)

                def exp(V, s):
                    act.wait_ge(s_sh, V + 1)
                    at_least(act, s_atT, V)
                    for g in range(GPT):
                        act.activation(attn[g * N:(g + 1) * N, :, g * N:(g + 1) * N],
                                       shifted2[g * N:(g + 1) * N], ACT.Exp).then_inc(s_at, 1)

                def keep_attn(V, s):
                    act.wait_ge(s_atT, V + 1)
                    at_least(act, s_agg, V)
                    act.copy(attn_T[:].rearrange("p t i -> p (t i)"), ATT_T[:]).then_inc(s_atk, 1)

                def norm_n(V, s):
                    act.wait_ge(s_nma, V + 1)
                    for t in range(TG):
                        act.activation(n_tok[:, t, :], n_tok[:, t, :], ACT.Identity, bias=nm_a[:, t:t + 1],
                                       scale=rs_a[:, t:t + 1]).then_inc(s_n, 1)

                def split_n(V, s):
                    for k in range(KD):
                        act.wait_ge(s_nT, KD * V + k + 1)
                        act.copy(nT_hi[:, s % 2, k, :], NT_B[k][:]).then_inc(s_nhi, 1)

                def before():
                    act.wait_ge(s_zero, 1)
                    exp(0, 0)
                    keep_attn(0, 0)
                    norm_n(0, 0)
                    split_n(0, 0)

                def lap(i, last):
                    for s in range(SLOTS):
                        U, nxt = i * SLOTS + s, not (last and s == SLOTS - 1)
                        V = U + 1
                        for c in range(CF):
                            gelu(U, s, c)
                            if s > 0 and c in (3, 4):
                                norm_y(U - 1, range(2 * c - 6, 2 * c - 4))
                            if nxt and c == 4:
                                exp(V, s + 1)
                            if nxt and c == 5:
                                keep_attn(V, s + 1)
                        if nxt:
                            norm_n(V, s + 1)
                            split_n(V, s + 1)
                    norm_y(i * SLOTS + SLOTS - 1, range(TG))

                laps(act, before, lap)

            @blk.gpsimd
            def _(pool):
                pool.sem_inc(s_x, 2)

                def rstd_of(dst, src, wait, count, done):
                    pool.wait_ge(wait, count)
                    pool.tensor_tensor(dst[:], src[:], minus_half[:], ALU.pow).then_inc(done, 1)

                def new_x(U, s):
                    l, g = layer_group(s)
                    pool.wait_ge(s_yn, TG * (U + 1))
                    xg = x_cur[:, g]
                    pool.tensor_tensor(xg, y_tok[:], g2_row[:, l].unsqueeze(1).broadcast_to([P, TG, D]), ALU.mult).then_inc(s_x, 1)
                    pool.wait_ge(s_x, 2 * U + 3)
                    pool.tensor_tensor(xg, xg, beta2_row[:, l].unsqueeze(1).broadcast_to([P, TG, D]), ALU.add).then_inc(s_x, 1)

                def finish(i, s):
                    l, g = layer_group(s)
                    U = i * SLOTS + s
                    pool.wait_ge(s_x, 2 * U + 4)
                    pool.wait_ge(s_res[g % 2], 16 * (i * (QG // 2) + g // 2 + 1))
                    pool.tensor_tensor(x_fin[:, g % 2], x_fin[:, g % 2], x_cur[:, g], ALU.add).then_inc(s_fin, 1)

                def post(i, s):
                    U = i * SLOTS + s
                    rstd_of(rs_f, ve_f, s_mvf, (TG + 1) * (U + 1), s_rsf)
                    new_x(U, s)
                    if layer_group(s)[0] == L - 1:
                        finish(i, s)

                def make_base(V, s):
                    l, g = layer_group(s)
                    pool.wait_ge(s_n, TG * (V + 1))
                    pool.tensor_tensor(base[:, s % 2], n_tok[:], g1_row[:, l].unsqueeze(1).broadcast_to([P, TG, D]),
                                       ALU.mult).then_inc(s_base, 1)
                    pool.wait_ge(s_base, 2 * V + 1)
                    pool.tensor_tensor(base[:, s % 2], base[:, s % 2], c1_row[:, l].unsqueeze(1).broadcast_to([P, TG, D]),
                                       ALU.add).then_inc(s_base, 1)

                def before():
                    rstd_of(rs_a, ve_a, s_mva, TG + 1, s_rsa)
                    make_base(0, 0)

                def lap(i, last):
                    for s in range(SLOTS):
                        U, nxt = i * SLOTS + s, not (last and s == SLOTS - 1)
                        V = U + 1
                        if s > 0:
                            post(i, s - 1)
                        if nxt:
                            rstd_of(rs_a, ve_a, s_mva, (TG + 1) * (V + 1), s_rsa)
                            make_base(V, s + 1)
                    post(i, SLOTS - 1)

                laps(pool, before, lap)

            @blk.vector
            def _(dve):
                dve.memset(attn[:], 0.0).then_inc(s_zero, 1)
                dve.sem_inc(s_y, TG)
                score = Steps(dve, s_sc, 7)

                def split(U, c):
                    dve.wait_ge(s_gelu, CF * U + c + 3)
                    dve.tensor_tensor(hid_lo[:, c % RING, :], hid[:, c % RING, :], hid_hi[:, c % RING, :].bitcast(F32),
                                      ALU.subtract).then_inc(s_split, 1)

                def take_y(U, s):
                    dve.wait_ge(s_ff, CF * (U + 1) + RING)
                    dve.wait_ge(s_base, 2 * U + 2)
                    dve.wait_ge(s_x, 2 * U + 1)
                    for t in range(TG):
                        dve.tensor_tensor(y_tok[:, t, :], FF[t // 2][:, (t % 2) * D:(t % 2 + 1) * D], base[:, s % 2, t, :],
                                          ALU.add).then_inc(s_y, 1)

                def stats_y(U, s):
                    for t in range(TG):
                        dve.wait_ge(s_y, TG * (U + 1) + t + 1)
                        dve.bn_stats(st_f[:, t, :], y_tok[:, t, :]).then_inc(s_stf, 1)
                    pause(dve, s_stf, TG * U + TG, s_own)
                    for t in range(TG):
                        dve.bn_aggr(mv_f[:, t, :], st_f[:, t, :]).then_inc(s_mvf, 1)
                    dve.wait_ge(s_mvf, (TG + 1) * U + TG)
                    dve.tensor_scalar(ve_f[:].unsqueeze(2), mv_f[:, :, 1:2], EPS, None, ALU.add).then_inc(s_mvf, 1)

                def shift_y(U, s):
                    dve.wait_ge(s_rsf, U + 1)
                    dve.scalar_tensor_tensor(nm_f[:].unsqueeze(2), mv_f[:, :, 0:1], -1.0, rs_f[:].unsqueeze(2),
                                             ALU.mult, ALU.mult).then_inc(s_nmf, 1)

                def dots_of(i, s, ts):
                    l, g = layer_group(s)
                    V = i * SLOTS + s
                    if ts[0] == 0:
                        if l == 0:
                            dve.wait_ge(s_in[g], 32 * (i + s // SLOTS + 1))
                        else:
                            dve.wait_ge(s_x, 2 * (V - QG) + 4)
                    for t in ts:
                        for j, dst in enumerate((s_src, s_dst)):
                            n = 2 * t + j
                            at_least(dve, s_dots, 8 * V + n)
                            dve.tensor_tensor_reduce(dots[:], x_cur[:, g, t, :], att_row[:, l, j, :], 1.0, 0.0,
                                                     ALU.mult, ALU.add, dst[:, t:t + 1]).then_inc(s_dots, 1)

                def diagonal(i, s):
                    l, g = layer_group(s)
                    V = i * SLOTS + s
                    dve.wait_ge(s_dots, 2 * TG * (V + 1))
                    at_least(dve, s_spread, V)
                    dve.tensor_tensor(diag2[:], node_of[:].unsqueeze(1).broadcast_to([P, TG, N]),
                                      s_dst[:].unsqueeze(2).broadcast_to([P, TG, N]), ALU.mult).then_inc(s_dg, 1)
                    score.unit(V)
                    score.done(dve.tensor_scalar(src_b[:], s_src[:], attb_row[:, l:l + 1], None, ALU.add))
                    if l == 0:
                        score.done(dve.tensor_tensor(mask_sum[:], adj_raw[:, g], node_of[:].unsqueeze(1).broadcast_to([P, TG, N]),
                                                     ALU.add))
                        score.wait()
                        score.done(dve.tensor_scalar(mask[:, g], mask_sum[:], 0.0, NEG, ALU.is_le, ALU.mult))
                        score.wait()
                    else:
                        score.k += 2
                        dve.sem_inc(s_sc, 2)

                def scores(i, s):
                    l, g = layer_group(s)
                    V = i * SLOTS + s
                    score.wait()
                    dve.wait_ge(s_spread, V + 1)
                    score.done(dve.tensor_tensor(masked2[:], SPREAD[:, 0:TG * N].rearrange("p (t j) -> p t j", t=TG), mask[:, g],
                                                 ALU.add))
                    score.wait()
                    score.done(dve.tensor_reduce(top2[:], masked2[:], AX, ALU.max))
                    dve.tensor_tensor(scored2[:], masked2[:], src_b[:].unsqueeze(2).broadcast_to([P, TG, N]),
                                      ALU.add).then_inc(s_scd, 1)
                    score.wait()
                    score.done(dve.tensor_tensor(top2_s[:], top2[:], src_b[:], ALU.add))
                    dve.wait_ge(s_scd, 2 * V + 1)
                    dve.scalar_tensor_tensor(leaky2[:], scored2[:], SLOPE, scored2[:], ALU.mult, ALU.max).then_inc(s_scd, 1)
                    score.wait()
                    score.done(dve.scalar_tensor_tensor(top2_l[:], top2_s[:], SLOPE, top2_s[:], ALU.mult, ALU.max))
                    score.wait()
                    dve.wait_ge(s_scd, 2 * V + 2)
                    at_least(dve, s_at, GPT * V)
                    dve.tensor_tensor(shifted2[:], leaky2[:], top2_l[:].unsqueeze(2).broadcast_to([P, TG, N]),
                                      ALU.subtract).then_inc(s_sh, 1)

                def sums(V):
                    dve.wait_ge(s_at, GPT * (V + 1))
                    dve.tensor_reduce(row_sum[:], attn[:], AX, ALU.add).then_inc(s_inv, 1)
                    dve.wait_ge(s_inv, 2 * V + 1)
                    dve.reciprocal(row_inv[:], row_sum[:]).then_inc(s_inv, 1)

                def residual(i, s):
                    l, g = layer_group(s)
                    V = i * SLOTS + s
                    dve.wait_ge(s_agg, V + 1)
                    dve.wait_ge(s_inv, 2 * V + 2)
                    at_least(dve, s_nT, KD * V)
                    at_least(dve, s_base, 2 * V - 1)
                    for t in range(TG):
                        dve.scalar_tensor_tensor(n_tok[:, t, :], AGG[t // 2][:, (t % 2) * D:(t % 2 + 1) * D], row_inv[:, t:t + 1],
                                                 x_cur[:, g, t, :], ALU.mult, ALU.add).then_inc(s_u, 1)

                def stats_n(V):
                    for t in range(TG):
                        dve.wait_ge(s_u, TG * V + t + 1)
                        dve.bn_stats(st_a[:, t, :], n_tok[:, t, :]).then_inc(s_sta, 1)
                    pause(dve, s_sta, TG * V + TG, s_own)
                    for t in range(TG):
                        dve.bn_aggr(mv_a[:, t, :], st_a[:, t, :]).then_inc(s_mva, 1)
                    dve.wait_ge(s_mva, (TG + 1) * V + TG)
                    dve.tensor_scalar(ve_a[:].unsqueeze(2), mv_a[:, :, 1:2], EPS, None, ALU.add).then_inc(s_mva, 1)

                def shift_n(V):
                    dve.wait_ge(s_rsa, V + 1)
                    dve.scalar_tensor_tensor(nm_a[:].unsqueeze(2), mv_a[:, :, 0:1], -1.0, rs_a[:].unsqueeze(2),
                                             ALU.mult, ALU.mult).then_inc(s_nma, 1)

                def split_n(V, s):
                    for k in range(KD):
                        dve.wait_ge(s_nhi, KD * V + k + 1)
                        dve.tensor_tensor(nT_lo[:, s % 2, k, :], NT_B[k][:], nT_hi[:, s % 2, k, :].bitcast(F32),
                                          ALU.subtract).then_inc(s_nlo, 1)

                def before():
                    dots_of(0, 0, range(TG))
                    diagonal(0, 0)
                    scores(0, 0)
                    sums(0)
                    residual(0, 0)
                    stats_n(0)
                    shift_n(0)
                    split_n(0, 0)

                def lap(i, last):
                    for s in range(SLOTS):
                        U, nxt = i * SLOTS + s, not (last and s == SLOTS - 1)
                        V = U + 1
                        if s > 0:
                            take_y(U - 1, s - 1)
                        split(U, 0)
                        if nxt:
                            dots_of(i, s + 1, range(0, 2))
                        split(U, 1)
                        if nxt:
                            dots_of(i, s + 1, range(2, 4))
                            diagonal(i, s + 1)
                        split(U, 2)
                        if s > 0:
                            stats_y(U - 1, s - 1)
                        if nxt:
                            scores(i, s + 1)
                        if s > 0:
                            shift_y(U - 1, s - 1)
                        split(U, 3)
                        split(U, 4)
                        if nxt:
                            sums(V)
                        split(U, 5)
                        if nxt:
                            residual(i, s + 1)
                        split(U, 6)
                        if nxt:
                            stats_n(V)
                        split(U, 7)
                        if nxt:
                            shift_n(V)
                            split_n(V, s + 1)
                    E = i * SLOTS + SLOTS - 1
                    take_y(E, SLOTS - 1)
                    stats_y(E, SLOTS - 1)
                    shift_y(E, SLOTS - 1)

                laps(dve, before, lap)

_INS = ['x', 'adj', 'L0_gnn_W_proj', 'L0_gnn_W_att', 'L0_gnn_b_att', 'L1_gnn_attn_w', 'L1_gnn_attn_b', 'L1_gnn_W1',
        'L1_gnn_b1', 'L1_gnn_W2', 'L1_gnn_b2', 'L1_gnn_g1', 'L1_gnn_beta1', 'L1_gnn_g2', 'L1_gnn_beta2']
_OUTS = [((128, 64, 256), 'float32')]


def kernel(**inputs):
    import numpy as _np
    import concourse.bacc as _bacc
    from concourse import mybir as _mybir
    from concourse.bass_utils import run_bass_kernel_spmd as _run

    nc = _bacc.Bacc("TRN2", target_bir_lowering=False, num_devices=1)
    arrays, args = {}, []
    for name in _INS:
        a = _np.ascontiguousarray(inputs[name])
        arrays[f"in_{name}_dram"] = a
        args.append(nc.dram_tensor(f"in_{name}_dram", a.shape, _mybir.dt.from_np(a.dtype), kind="ExternalInput").ap())
    for i, (shape, dtype) in enumerate(_OUTS):
        dt = _mybir.dt.from_np(_np.dtype(dtype))
        args.append(nc.dram_tensor(f"out_{i}_dram", shape, dt, kind="ExternalOutput").ap())
    graph_net(nc, *args)
    r = _run(nc, [arrays], core_ids=[0])
    got = tuple(r.results[0][f"out_{i}_dram"] for i in range(len(_OUTS)))
    return got[0]
```

```python
from contextlib import ExitStack

import concourse.bass as bass
from concourse import mybir

F32 = mybir.dt.float32
F32R = mybir.dt.float32r
I32 = mybir.dt.int32
ALU = mybir.AluOpType
ACT = mybir.ActivationFunctionType
AX = mybir.AxisListType.X

P = 128
NEG = -1e30
SLOPE = 0.2
EPS = 1e-5


def at_least(eng, sem, value):
    if not isinstance(value, int) or value > 0:
        eng.wait_ge(sem, value)


def pause(eng, sem, value, own):
    if not isinstance(value, int) or value > 0:
        eng.wait_ge(sem, value)
        eng.sem_inc(own, 1)


class Steps:

    def __init__(self, eng, sem, per):
        self.eng, self.sem, self.per, self.base, self.k = eng, sem, per, 0, 0

    def unit(self, n):
        assert self.k in (0, self.per), self.k
        self.base, self.k = n * self.per, 0

    def done(self, instruction):
        self.k += 1
        instruction.then_inc(self.sem, 1)

    def wait(self):
        self.eng.wait_ge(self.sem, self.base + self.k)


def graph_net(nc, x, adj, w_proj, w_att, b_att, attn_w, attn_b, w1, b1, w2, b2, g1, beta1, g2, beta2, out):
    B, N, D = x.shape
    H, K2 = w_att.shape
    HK = K2 // 2
    L, _, F = w1.shape
    NT = B * N // P
    GPT = P // N
    KD = D // P
    CF = F // P
    TG = 4
    NG = NT // TG
    TOK = TG * P
    QG = 4
    LAPS = NG // QG
    SLOTS = L * QG
    WC = D + 2 * H
    HC = HK + 1
    RING = 2

    x_v = x.rearrange("(t g) n d -> (g n) t d", g=GPT)
    out_v = out.rearrange("(t g) n d -> (g n) t d", g=GPT)
    adj_v = adj.rearrange("(t g) i j -> (g i) t j", g=GPT)
    res_d = nc.dram_tensor("first_block_out", (P, NT, D), F32, kind="Internal").ap()
    act_d = nc.dram_tensor("second_block_in", (P, NT, D), F32, kind="Internal").ap()

    def row(ap, n):
        return ap.rearrange("(a n) -> a n", a=1).broadcast_to([P, n])

    ctx = ExitStack()
    with ctx:
        def sb(name, shape, dt=F32, where=None):
            return (where or ctx).enter_context(nc.sbuf_tensor(name, shape, dt))

        def sem(name):
            return ctx.enter_context(nc.semaphore(name))

        bank = [ctx.enter_context(nc.psum_tensor(f"bank{i}", [P, 512], F32)) for i in range(8)]

        ident = sb("ident", [P, P])
        node_of = sb("node_of", [P, N])
        same_graph = sb("same_graph", [P, P])
        minus_half = sb("minus_half", [P, TG])
        w1_hi, w1_lo = (sb(n, [P, L, KD, F], F32R) for n in ("w1_hi", "w1_lo"))
        w2_hi, w2_lo = (sb(n, [P, L, CF, D], F32R) for n in ("w2_hi", "w2_lo"))
        b1_col = sb("b1_col", [P, L, CF])
        g1_row, c1_row, g2_row, beta2_row = (sb(n, [P, L, D]) for n in ("g1_row", "c1_row", "g2_row", "beta2_row"))
        att_row = sb("att_row", [P, L, 2, D])
        attb_row = sb("attb_row", [P, L])

        setup = ExitStack()
        projection = ctx.enter_context(ExitStack())
        wcat_hi, wcat_lo = (sb(n, [P, KD, WC], F32R, where=projection) for n in ("wcat_hi", "wcat_lo"))
        batt_row = sb("batt_row", [P, H], where=projection)
        with setup:
            stage = sb("stage", [P, 2, KD * F], where=setup)
            wcat = sb("wcat", [P, KD, WC], where=setup)
            watt_row = sb("watt_row", [P, 2, H, HK], where=setup)
            prod = sb("prod", [P, H, HK], where=setup)
            b1_raw = sb("b1_raw", [P, L, CF], where=setup)
            g1_col, beta1_col = (sb(n, [P, L, KD], where=setup) for n in ("g1_col", "beta1_col"))
            b2_row = sb("b2_row", [P, L, D], where=setup)
            s_w = [sem(f"stage_loaded{i}") for i in range(2)]
            s_col, s_rows, s_cat = sem("columns_loaded"), sem("rows_loaded"), sem("wcat_loaded")
            s_fill, s_const = sem("consts_filled"), sem("consts_made")
            s_bias, s_scaled = sem("bias_products"), sem("weights_scaled")
            s_hi, s_lo, s_su = sem("weight_hi"), sem("weight_lo"), sem("setup_vector")
            s_b1, s_same = sem("bias_kept"), sem("same_graph_made")
            JOBS = [(l, which) for l in range(L) for which in (1, 2)]
            blk = setup.enter_context(nc.Block())

            @blk.sync
            def _(sp):
                with nc.allow_non_contiguous_dma(reason="small columns"):
                    for k in range(KD):
                        sp.dma_start(wcat[:, k, 0:D], w_proj[k * P:(k + 1) * P, :]).then_inc(s_cat, 16)
                    for i in range(2):
                        sp.dma_start(watt_row[:, i], w_att[:, i * HK:(i + 1) * HK].rearrange("(a h) k -> a h k", a=1)
                                     .broadcast_to([P, H, HK])).then_inc(s_cat, 16)
                    sp.dma_start(b1_raw[:], b1.rearrange("l (c p) -> p l c", p=P)).then_inc(s_col, 16)
                    sp.dma_start(g1_col[:], g1.rearrange("l (c p) -> p l c", p=P)).then_inc(s_col, 16)
                    sp.dma_start(beta1_col[:], beta1.rearrange("l (c p) -> p l c", p=P)).then_inc(s_col, 16)
                    for n, (l, which) in enumerate(JOBS):
                        if n >= 2:
                            sp.wait_ge(s_lo, n - 1 + 1)
                        if which == 1:
                            sp.dma_start(stage[:, n % 2, :].rearrange("p (c f) -> p c f", c=KD),
                                         w1[l].rearrange("(c p) f -> p c f", p=P)).then_inc(s_w[n % 2], 16)
                        else:
                            sp.dma_start(stage[:, n % 2, :].rearrange("p (c d) -> p c d", c=CF),
                                         w2[l].rearrange("(c p) d -> p c d", p=P)).then_inc(s_w[n % 2], 16)

            @blk.gpsimd
            def _(pool):
                pool.memset(ident[:], 0.0).then_inc(s_fill, 1)
                pool.memset(node_of[:], 0.0).then_inc(s_fill, 1)
                pool.memset(minus_half[:], -0.5).then_inc(s_const, 1)
                pool.wait_ge(s_fill, 2)
                pool.affine_select(out=ident[:], in_=ident[:], compare_op=ALU.not_equal, fill=1.0, base=0,
                                   pattern=[[-1, P]], channel_multiplier=1).then_inc(s_const, 1)
                pool.affine_select(out=node_of[:], in_=node_of[:], compare_op=ALU.not_equal, fill=1.0, base=0,
                                   pattern=[[-1, N]], channel_multiplier=1).then_inc(s_fill, 1)
                pool.wait_ge(s_fill, 3)
                pool.affine_select(out=node_of[:], in_=node_of[:], compare_op=ALU.not_equal, fill=1.0, base=-N,
                                   pattern=[[-1, N]], channel_multiplier=1).then_inc(s_const, 1)
                with nc.allow_non_contiguous_dma(reason="broadcast rows"):
                    for l in range(L):
                        for dst, src in ((g1_row, g1), (c1_row, beta1), (g2_row, g2), (beta2_row, beta2), (b2_row, b2)):
                            pool.dma_start(dst[:, l, :], row(src[l], D)).then_inc(s_rows, 16)
                        pool.dma_start(att_row[:, l].rearrange("p a d -> p (a d)"), row(attn_w[l], 2 * D)).then_inc(s_rows, 16)
                    pool.dma_start(attb_row[:], row(attn_b, L)).then_inc(s_rows, 16)
                    pool.dma_start(batt_row[:], row(b_att, H)).then_inc(s_rows, 16)
                pool.wait_ge(s_rows, 16 * (6 * L + 2))
                pool.tensor_tensor(c1_row[:], c1_row[:], b2_row[:], ALU.add).then_inc(s_const, 1)

            @blk.tensor
            def _(pe):
                pe.wait_ge(s_col, 48)
                for l in range(L):
                    n = 2 * l
                    pe.wait_ge(s_w[0], 16 * (l + 1))
                    for c in range(CF):
                        for k in range(KD):
                            mm = pe.matmul(bank[0][:, l * CF + c:l * CF + c + 1],
                                           stage[:, n % 2, k * F + c * P:k * F + (c + 1) * P], beta1_col[:, l, k:k + 1],
                                           start=(k == 0), stop=(k == KD - 1))
                    mm.then_inc(s_bias, 1)

            @blk.scalar
            def _(act):
                act.wait_ge(s_su, 2 * KD * 2)
                act.copy(wcat_hi[:], wcat[:]).then_inc(s_hi, 1)
                for n, (l, which) in enumerate(JOBS):
                    if which == 1:
                        act.wait_ge(s_scaled, (l + 1) * KD)
                        act.copy(w1_hi[:, l].rearrange("p c f -> p (c f)"), stage[:, n % 2, :]).then_inc(s_hi, 1)
                    else:
                        act.wait_ge(s_w[1], 16 * (l + 1))
                        act.copy(w2_hi[:, l].rearrange("p c f -> p (c f)"), stage[:, n % 2, :]).then_inc(s_hi, 1)

            @blk.vector
            def _(dve):
                dve.memset(same_graph[:], 0.0).then_inc(s_same, 1)
                dve.wait_ge(s_same, 1)
                for g in range(GPT):
                    dve.memset(same_graph[g * N:(g + 1) * N, g * N:(g + 1) * N], 1.0).then_inc(s_same, 1)
                dve.wait_ge(s_cat, 16 * (KD + 2))
                done = 0
                for k in range(KD):
                    for i in range(2):
                        if done:
                            dve.wait_ge(s_su, done)
                        dve.tensor_tensor(prod[:], wcat[:, k, 0:D].rearrange("p (h k) -> p h k", h=H), watt_row[:, i],
                                          ALU.mult).then_inc(s_su, 1)
                        dve.wait_ge(s_su, done + 1)
                        dve.tensor_reduce(wcat[:, k, D + i * H:D + (i + 1) * H], prod[:], AX, ALU.add).then_inc(s_su, 1)
                        done += 2
                dve.wait_ge(s_hi, 1)
                dve.tensor_tensor(wcat_lo[:], wcat[:], wcat_hi[:].bitcast(F32), ALU.subtract).then_inc(s_lo, 1)
                dve.wait_ge(s_col, 48)
                for n, (l, which) in enumerate(JOBS):
                    if which == 1:
                        dve.wait_ge(s_bias, l + 1)
                        dve.tensor_tensor(b1_col[:, l], bank[0][:, l * CF:(l + 1) * CF], b1_raw[:, l], ALU.add).then_inc(s_b1, 1)
                        for k in range(KD):
                            w = stage[:, n % 2, k * F:(k + 1) * F]
                            dve.tensor_scalar(w, w, g1_col[:, l, k:k + 1], None, ALU.mult).then_inc(s_scaled, 1)
                        dve.wait_ge(s_scaled, (l + 1) * KD)
                        hi, lo = w1_hi, w1_lo
                    else:
                        hi, lo = w2_hi, w2_lo
                    dve.wait_ge(s_hi, n + 2)
                    dve.tensor_tensor(lo[:, l].rearrange("p c f -> p (c f)"), stage[:, n % 2, :],
                                      hi[:, l].rearrange("p c f -> p (c f)").bitcast(F32), ALU.subtract).then_inc(s_lo, 1)
                dve.wait_ge(s_lo, len(JOBS) + 1)

        first = ExitStack()
        with first:
            XR = 16
            xin = sb("xin", [P, XR, D], where=first)
            adjin = sb("adjin", [P, XR, N], I32, where=first)
            hrelu = sb("hrelu", [P, 2, D], where=first)
            hT_hi, hT_lo = (sb(n, [P, 2, D], F32R, where=first) for n in ("hT_hi", "hT_lo"))
            xh = sb("xh", [P, 4, H, HC], where=first)
            a_src = sb("a_src", [P, 4, H], where=first)
            a_dst = sb("a_dst", [P, 4, H], where=first)
            dst_diag = sb("dst_diag", [P, 2, H, N], where=first)
            no_edge = sb("no_edge", [P, N], where=first)
            masked, scored, leaky, shifted = (sb(n, [P, H, N], where=first) for n in ("masked", "scored", "leaky", "shifted"))
            top, top_s, top_l = (sb(n, [P, H], where=first) for n in ("top", "top_s", "top_l"))
            weights = sb("weights", [P, H, P], where=first)
            weights_T = sb("weights_T", [P, 2, H, P], where=first)
            inv = sb("inv", [P, H], where=first)
            headout = sb("headout", [P, D], where=first)
            x_res = sb("x_res", [P, 8, D], where=first)
            x_act = sb("x_act", [P, 8, D], where=first)
            stats = sb("stats", [P, 2, 6], where=first)
            mv = sb("mv", [P, 4, 2, 2], where=first)
            vare, rstd, nmr = (sb(n, [P, 4, 2], where=first) for n in ("vare", "rstd", "nmr"))

            q_own, q_own_sp, q_ld, q_s, q_vs, q_vh = sem("q_paused"), sem("q_sync_paused"), sem("tiles_loaded"), sem("q_stats"), sem("q_score_steps"), sem("q_heads_steps")
            q_st = sem("first_stored")
            q_zero = sem("first_filled")
            q_mv, q_rs, q_nmr, q_h = sem("q_mean_var"), sem("q_rstd"), sem("q_shift"), sem("q_h")
            q_tr, q_hi, q_lo = sem("q_hT"), sem("q_hT_hi"), sem("q_hT_lo")
            q_xp, q_xh, q_asd, q_diag = sem("q_proj"), sem("q_xh"), sem("q_src_dst"), sem("q_diag")
            q_bc, q_msk, q_sc, q_d, q_e = sem("q_dst_spread"), sem("q_masked"), sem("q_scored"), sem("q_shifted"), sem("q_weights")
            q_wt, q_ev, q_ag = sem("q_weights_T"), sem("q_weights_T_kept"), sem("q_heads")
            q_res, q_mean, q_act = sem("q_res"), sem("q_mean"), sem("q_act")
            blk = first.enter_context(nc.Block())

            HEAD, LAG = 16, 11

            def steps(eng, step):
                for tau in range(HEAD):
                    step(tau, tau)
                with eng.Fori(HEAD // 4, NT // 4) as i:
                    for t in range(4):
                        step(i * 4 + t, t)
                for tau in range(NT, NT + LAG):
                    step(tau, tau)

            def has(T):
                return not isinstance(T, int) or 0 <= T < NT

            def counted(S):
                return not isinstance(S, int) or 0 <= S < NT + 9

            @blk.sync
            def _(sp):
                def load_group(g, part):
                    pause(sp, q_ld, 32 * g, q_own_sp)
                    sp.dma_start(xin[:, part * 4:part * 4 + 4, :], x_v[:, bass.ts(g, 4), :]).then_inc(q_ld, 16)
                    sp.dma_start(adjin[:, part * 4:part * 4 + 4, :], adj_v[:, bass.ts(g, 4), :]).then_inc(q_ld, 16)

                def store_group(g, half):
                    pause(sp, q_res, 4 * g + 4, q_own_sp)
                    pause(sp, q_act, 4 * g + 4, q_own_sp)
                    pause(sp, q_st, 32 * g, q_own_sp)
                    sp.dma_start(res_d[:, bass.ts(g, 4), :], x_res[:, half * 4:half * 4 + 4, :]).then_inc(q_st, 16)
                    sp.dma_start(act_d[:, bass.ts(g, 4), :], x_act[:, half * 4:half * 4 + 4, :]).then_inc(q_st, 16)

                for g in range(4):
                    load_group(g, g)
                with sp.Fori(0, NG // 4 - 1) as i:
                    for part in range(4):
                        pause(sp, q_res, i * 16 + (part * 4 + 4), q_own_sp)
                        load_group(i * 4 + (part + 4), part)
                        store_group(i * 4 + part, part % 2)
                for g in range(NG - 4, NG):
                    store_group(g, g % 2)
                sp.wait_ge(q_st, 32 * NG)

            @blk.tensor
            def _(pe):
                def step(tau, t):
                    T, r = tau - 6, (t - 6)
                    if has(T):
                        pe.wait_ge(q_diag, T + 1)
                        at_least(pe, q_msk, T)
                        pe.matmul(bank[4][:], same_graph[:], dst_diag[:, r % 2].rearrange("p h j -> p (h j)"),
                                  start=True, stop=True).then_inc(q_bc, 1)
                    T, r = tau - 3, (t - 3)
                    if has(T):
                        pe.wait_ge(q_h, T + 1)
                        at_least(pe, q_lo, T - 1)
                        for k in range(KD):
                            mm = pe.transpose(bank[r % 2][:, k * P:(k + 1) * P], hrelu[:, r % 2, k * P:(k + 1) * P], ident[:])
                        mm.then_inc(q_tr, 1)
                    T, r = tau - 8, (t - 8)
                    if has(T):
                        pe.wait_ge(q_ev, 2 * T + 2)
                        pe.wait_ge(q_xh, T + 1)
                        at_least(pe, q_vh, 2 * T)
                        for h in range(H):
                            mm = pe.matmul(bank[7][:, h * HC:(h + 1) * HC], weights_T[:, r % 2, h, :],
                                           xh[:, r % 4, h, :], start=True, stop=True)
                        mm.then_inc(q_ag, 1)
                    T, r = tau - 4, (t - 4)
                    if has(T):
                        pe.wait_ge(q_lo, T + 1)
                        at_least(pe, q_xh, T - 1)
                        at_least(pe, q_asd, 2 * (T - 1))
                        for k in range(KD):
                            for p, (a, w) in enumerate(((hT_hi, wcat_hi), (hT_hi, wcat_lo), (hT_lo, wcat_hi))):
                                mm = pe.matmul(bank[2 + r % 2][:, 0:WC], a[:, r % 2, k * P:(k + 1) * P], w[:, k, :],
                                               start=(k == 0 and p == 0), stop=(k == KD - 1 and p == 2))
                        mm.then_inc(q_xp, 1)
                    T, r = tau - 7, (t - 7)
                    if has(T):
                        pe.wait_ge(q_e, 2 * T + 2)
                        at_least(pe, q_ev, 2 * T)
                        for h in range(H):
                            mm = pe.transpose(bank[5 + h // 4][:, (h % 4) * P:(h % 4 + 1) * P], weights[:, h, :], ident[:])
                        mm.then_inc(q_wt, 1)

                steps(pe, step)

            @blk.scalar
            def _(act):
                def step(tau, t):
                    T, r = tau - 3, (t - 3)
                    if has(T):
                        act.wait_ge(q_tr, T + 1)
                        at_least(act, q_xp, T - 1)
                        act.copy(hT_hi[:, r % 2, :], bank[r % 2][:, 0:D]).then_inc(q_hi, 1)
                    T, r = tau - 2, (t - 2)
                    if has(T):
                        act.wait_ge(q_nmr, T + 1)
                        at_least(act, q_tr, T - 1)
                        act.activation(hrelu[:, r % 2, :], xin[:, T % XR, :], ACT.Relu,
                                       bias=nmr[:, r % 4, 0:1], scale=rstd[:, r % 4, 0:1]).then_inc(q_h, 1)
                    T, r = tau - 4, (t - 4)
                    if has(T):
                        act.wait_ge(q_xp, T + 1)
                        at_least(act, q_ag, T - 3)
                        if isinstance(T, int) and T == 0:
                            act.wait_ge(q_zero, 2)
                        act.copy(xh[:, r % 4, :, 0:HK], bank[2 + r % 2][:, 0:D].rearrange("p (h k) -> p h k", h=H)).then_inc(q_xh, 1)
                    T, r = tau - 7, (t - 7)
                    if has(T):
                        act.wait_ge(q_wt, T + 1)
                        at_least(act, q_ag, T - 1)
                        for b in range(2):
                            act.copy(weights_T[:, r % 2, 4 * b:4 * b + 4, :].rearrange("p h i -> p (h i)"),
                                     bank[5 + b][:]).then_inc(q_ev, 1)
                    T, r = tau - 6, (t - 6)
                    if has(T):
                        act.wait_ge(q_d, T + 1)
                        at_least(act, q_wt, T)
                        if isinstance(T, int) and T == 0:
                            act.wait_ge(q_zero, 1)
                        for g in range(GPT):
                            act.activation(weights[g * N:(g + 1) * N, :, g * N:(g + 1) * N],
                                           shifted[g * N:(g + 1) * N], ACT.Exp).then_inc(q_e, 1)
                    T, r = tau - 11, (t - 11)
                    if has(T):
                        act.wait_ge(q_nmr, T + 10)
                        if r % 4 == 0:
                            at_least(act, q_st, 8 * (T - 4))
                        act.activation(x_act[:, T % 8, :],
                                       x_res[:, T % 8, :], ACT.Relu,
                                       bias=nmr[:, (r + 1) % 4, 1:2], scale=rstd[:, (r + 1) % 4, 1:2]).then_inc(q_act, 1)

                steps(act, step)

            @blk.gpsimd
            def _(pool):
                def step(tau, t):
                    T, r = tau - 5, (t - 5)
                    if has(T):
                        pool.wait_ge(q_asd, 2 * T + 2)
                        at_least(pool, q_bc, T - 1)
                        pool.tensor_tensor(dst_diag[:, r % 2], node_of[:].unsqueeze(1).broadcast_to([P, H, N]),
                                           a_dst[:, r % 4, :].unsqueeze(2).broadcast_to([P, H, N]), ALU.mult).then_inc(q_diag, 1)
                    T, r = tau - 6, (t - 6)
                    if has(T):
                        pool.wait_ge(q_msk, T + 1)
                        at_least(pool, q_d, T)
                        pool.tensor_tensor(scored[:], masked[:], a_src[:, r % 4, :].unsqueeze(2).broadcast_to([P, H, N]),
                                           ALU.add).then_inc(q_sc, 1)
                    T, r = tau - 8, (t - 8)
                    if has(T):
                        pool.wait_ge(q_vh, 2 * T + 2)
                        if r % 4 == 0:
                            at_least(pool, q_st, 8 * (T - 4))
                        pool.tensor_tensor(x_res[:, T % 8, :], headout[:], xin[:, T % XR, :], ALU.add).then_inc(q_res, 1)
                    S, r = tau - 1, (t - 1)
                    if counted(S):
                        pool.wait_ge(q_mv, S + 1)
                        at_least(pool, q_act, S - 12)
                        pool.tensor_tensor(rstd[:, r % 4, :], vare[:, r % 4, :], minus_half[:, 0:2], ALU.pow).then_inc(q_rs, 1)

                steps(pool, step)

            @blk.vector
            def _(dve):
                dve.memset(weights[:], 0.0).then_inc(q_zero, 1)
                dve.memset(xh[:, :, :, HK:HC], 1.0).then_inc(q_zero, 1)
                dve.memset(mv[:], 0.0).then_inc(q_zero, 1)
                dve.wait_ge(q_zero, 3)
                score = Steps(dve, q_vs, 5)
                heads = Steps(dve, q_vh, 2)

                def step(tau, t):
                    scores, r = tau - 6, (t - 6)
                    if has(scores):
                        score.unit(scores)
                        score.done(dve.tensor_scalar(no_edge[:], adjin[:, scores % XR, :], 0.0, NEG, ALU.is_le, ALU.mult))
                    S = tau - 2
                    if counted(S):
                        dve.wait_ge(q_rs, S + 1)
                        dve.scalar_tensor_tensor(nmr[:, (t - 2) % 4].unsqueeze(2), mv[:, (t - 2) % 4, :, 0:1], -1.0,
                                                 rstd[:, (t - 2) % 4].unsqueeze(2), ALU.mult, ALU.mult).then_inc(q_nmr, 1)
                    if has(tau):
                        if t % 4 == 0:
                            pause(dve, q_ld, 32 * (tau // 4 + 1), q_own)
                        bn = dve.bn_stats(stats[:, 0, :], xin[:, tau % XR, :])
                    if has(tau - 9):
                        pause(dve, q_res, tau - 8, q_own)
                        bn = dve.bn_stats(stats[:, 1, :], x_res[:, (tau - 9) % 8, :])
                    if counted(tau):
                        bn.then_inc(q_s, 1)
                    if has(scores):
                        score.wait()
                        dve.wait_ge(q_bc, scores + 1)
                        at_least(dve, q_sc, scores)
                        dve.tensor_tensor(masked[:], bank[4][:].rearrange("p (h j) -> p h j", h=H),
                                          no_edge[:].unsqueeze(1).broadcast_to([P, H, N]), ALU.add).then_inc(q_msk, 1)
                    T, r3 = tau - 3, (t - 3)
                    if has(T):
                        dve.wait_ge(q_hi, T + 1)
                        at_least(dve, q_xp, T - 1)
                        dve.tensor_tensor(hT_lo[:, r3 % 2, :], bank[r3 % 2][:, 0:D], hT_hi[:, r3 % 2, :].bitcast(F32),
                                          ALU.subtract).then_inc(q_lo, 1)
                    T8 = tau - 8
                    if has(T8):
                        heads.unit(T8)
                        dve.wait_ge(q_ag, T8 + 1)
                        G = bank[7][:, 0:H * HC].rearrange("p (h k) -> p h k", h=H)
                        heads.done(dve.reciprocal(inv[:].unsqueeze(2), G[:, :, HK:HC]))
                    if has(scores):
                        dve.wait_ge(q_msk, scores + 1)
                        score.done(dve.tensor_reduce(top[:], masked[:], AX, ALU.max))
                    if has(T8):
                        heads.wait()
                        at_least(dve, q_res, T8)
                        heads.done(dve.scalar_tensor_tensor(headout[:].rearrange("p (h k) -> p h k", h=H), G[:, :, 0:HK],
                                                            0.0, inv[:].unsqueeze(2).broadcast_to([P, H, HK]),
                                                            ALU.max, ALU.mult))
                    if counted(tau):
                        pause(dve, q_s, tau + 1, q_own)
                        for kind, T in ((0, tau), (1, tau - 9)):
                            if has(T):
                                last = dve.bn_aggr(mv[:, t % 4, kind, :], stats[:, kind, :])
                        last.then_inc(q_mean, 1)
                    if has(scores):
                        score.wait()
                        score.done(dve.tensor_tensor(top_s[:], top[:], a_src[:, r % 4, :], ALU.add))
                    if counted(tau):
                        dve.wait_ge(q_mean, tau + 1)
                        dve.tensor_scalar(vare[:, t % 4].unsqueeze(2), mv[:, t % 4, :, 1:2], EPS, None, ALU.add).then_inc(q_mv, 1)
                    if has(scores):
                        score.wait()
                        score.done(dve.scalar_tensor_tensor(top_l[:], top_s[:], SLOPE, top_s[:], ALU.mult, ALU.max))
                    if has(scores):
                        dve.wait_ge(q_sc, scores + 1)
                        score.done(dve.scalar_tensor_tensor(leaky[:], scored[:], SLOPE, scored[:], ALU.mult, ALU.max))
                    T, r4 = tau - 4, (t - 4)
                    if has(T):
                        dve.wait_ge(q_xh, T + 1)
                        at_least(dve, q_sc, T - 3)
                        at_least(dve, q_diag, T - 3)
                        X = bank[2 + r4 % 2]
                        dve.tensor_tensor(a_src[:, r4 % 4, :], X[:, D:D + H], batt_row[:], ALU.add).then_inc(q_asd, 1)
                        dve.tensor_copy(a_dst[:, r4 % 4, :], X[:, D + H:D + 2 * H]).then_inc(q_asd, 1)
                    if has(scores):
                        score.wait()
                        at_least(dve, q_e, 2 * scores)
                        dve.tensor_tensor(shifted[:], leaky[:], top_l[:].unsqueeze(2).broadcast_to([P, H, N]),
                                          ALU.subtract).then_inc(q_d, 1)

                steps(dve, step)
        projection.close()
        second = ExitStack()
        with second:
            x_cur = sb("x_cur", [P, QG, TG, D], where=second)
            x_fin = sb("x_fin", [P, 2, TG, D], where=second)
            adj_raw = sb("adj_raw", [P, QG, TG, N], I32, where=second)
            mask = sb("mask", [P, QG, TG, N], where=second)
            mask_sum = sb("mask_sum", [P, TG, N], where=second)
            dots = sb("dots", [P, D], where=second)
            s_src, s_dst = (sb(n, [P, TG], where=second) for n in ("s_src", "s_dst"))
            src_b = sb("src_b", [P, TG], where=second)
            diag2 = sb("diag2", [P, TG, N], where=second)
            masked2, scored2, leaky2, shifted2 = (sb(n, [P, TG, N], where=second)
                                                  for n in ("masked2", "scored2", "leaky2", "shifted2"))
            top2, top2_s, top2_l = (sb(n, [P, TG], where=second) for n in ("top2", "top2_s", "top2_l"))
            attn = sb("attn", [P, TG, P], where=second)
            attn_T = sb("attn_T", [P, TG, P], where=second)
            row_sum, row_inv = (sb(n, [P, TG], where=second) for n in ("row_sum", "row_inv"))
            n_tok = sb("n_tok", [P, TG, D], where=second)
            nT_hi, nT_lo = (sb(n, [P, 2, KD, TOK], F32R, where=second) for n in ("nT_hi", "nT_lo"))
            base = sb("base", [P, 2, TG, D], where=second)
            hid = sb("hid", [P, RING, TOK], where=second)
            hid_hi, hid_lo = (sb(n, [P, RING, TOK], F32R, where=second) for n in ("hid_hi", "hid_lo"))
            y_tok = sb("y_tok", [P, 2, TG, D], where=second)
            st_a, st_f = (sb(n, [P, TG, 6], where=second) for n in ("st_a", "st_f"))
            mv_a, mv_f = (sb(n, [P, TG, 2], where=second) for n in ("mv_a", "mv_f"))
            ve_a, ve_f, rs_a, rs_f, nm_a, nm_f = (sb(n, [P, TG], where=second)
                                                  for n in ("ve_a", "ve_f", "rs_a", "rs_f", "nm_a", "nm_f"))

            HID, FF = (bank[0], bank[1]), (bank[2], bank[3])
            SPREAD, ATT_T = bank[4], bank[5]
            AGG = NT_B = (bank[6], bank[7])

            s_in = [sem(f"group_loaded{g}") for g in range(QG)]
            s_res = [sem(f"res_loaded{i}") for i in range(2)]
            s_out = [sem(f"group_stored{i}") for i in range(2)]
            s_own, s_own_sp, s_zero, s_scd = sem("vector_paused"), sem("sync_paused"), sem("attn_zeroed"), sem("scores_leaky")
            s_hid, s_gelu, s_split, s_ff = sem("hidden"), sem("gelu"), sem("hidden_split"), sem("ff_chunk")
            s_y = sem("ff_read")
            s_stf, s_mvf, s_rsf, s_nmf, s_yn = sem("y_stats"), sem("y_mean_var"), sem("y_rstd"), sem("y_shift"), sem("y_norm")
            s_x, s_fin = sem("x_new"), sem("out_ready")
            s_dots, s_dg = sem("dots_done"), sem("dst_diagonal")
            s_spread, s_sc, s_sh, s_at = sem("dst_spread"), sem("score_steps"), sem("shifted_ready"), sem("attn_ready")
            s_atT, s_atk, s_agg = sem("attn_T_ready"), sem("attn_T_kept"), sem("aggregated")
            s_inv, s_u, s_sta, s_mva = sem("row_sums"), sem("residual_a"), sem("a_stats"), sem("a_mean_var")
            s_rsa, s_nma, s_n = sem("a_rstd"), sem("a_shift"), sem("n_ready")
            s_nT, s_nhi, s_nlo, s_base = sem("nT"), sem("nT_hi_ready"), sem("nT_lo_ready"), sem("base_ready")
            blk = second.enter_context(nc.Block())

            def laps(eng, before, lap):
                before()
                with eng.Fori(0, LAPS - 1) as i:
                    lap(i, False)
                lap(LAPS - 1, True)

            def layer_group(s):
                return s % SLOTS // QG, s % QG

            @blk.sync
            def _(sp):
                def load(lap, g):
                    n = lap * QG + g
                    sp.dma_start(x_cur[:, g], act_d[:, bass.ts(n, TG), :]).then_inc(s_in[g], 16)
                    sp.dma_start(adj_raw[:, g], adj_v[:, bass.ts(n, TG), :]).then_inc(s_in[g], 16)

                def load_res(lap, g):
                    n = lap * QG + g
                    sp.dma_start(x_fin[:, g % 2], res_d[:, bass.ts(n, TG), :]).then_inc(s_res[g % 2], 16)

                def before():
                    for g in range(QG):
                        load(0, g)
                    for g in range(2):
                        load_res(0, g)

                def refill(i, g, last):
                    if not last:
                        pause(sp, s_u, TG * (i * SLOTS + (L - 1) * QG + g + 1), s_own_sp)
                        load(i + 1, g)

                def put_out(i, g, last):
                    n = i * QG + g
                    pause(sp, s_fin, n + 3, s_own_sp)
                    sp.dma_start(out_v[:, bass.ts(n, TG), :], x_fin[:, g % 2]).then_inc(s_out[g % 2], 16)
                    pause(sp, s_out[g % 2], 16 * (i * (QG // 2) + g // 2 + 1), s_own_sp)
                    if g < 2:
                        load_res(i, g + 2)
                    elif not last:
                        load_res(i + 1, g - 2)

                def lap(i, last):
                    for g in range(3):
                        refill(i, g, last)
                    put_out(i, 0, last)
                    refill(i, 3, last)
                    for g in range(1, QG):
                        put_out(i, g, last)

                laps(sp, before, lap)

            @blk.tensor
            def _(pe):
                pe.sem_inc(s_ff, RING)

                def spread(V, s):
                    pe.wait_ge(s_dg, V + 1)
                    pe.matmul(SPREAD[:, 0:TG * N], same_graph[:], diag2[:].rearrange("p t j -> p (t j)"),
                              start=True, stop=True).then_inc(s_spread, 1)

                def turn_attn(V, s):
                    pe.wait_ge(s_at, GPT * (V + 1))
                    for t in range(TG):
                        mm = pe.transpose(ATT_T[:, t * P:(t + 1) * P], attn[:, t, :], ident[:])
                    mm.then_inc(s_atT, 1)

                def aggregate(V, s):
                    l, g = layer_group(s)
                    pe.wait_ge(s_atk, V + 1)
                    for t in range(TG):
                        mm = pe.matmul(AGG[t // 2][:, (t % 2) * D:(t % 2 + 1) * D], attn_T[:, t, :], x_cur[:, g, t, :],
                                       start=True, stop=True)
                    mm.then_inc(s_agg, 1)

                def turn_n(V, s):
                    for k in range(KD):
                        if k == 0:
                            pe.wait_ge(s_n, TG * (V + 1))
                        for t in range(TG):
                            mm = pe.transpose(NT_B[k][:, t * P:(t + 1) * P], n_tok[:, t, k * P:(k + 1) * P], ident[:])
                        mm.then_inc(s_nT, 1)

                def hidden(U, s, c):
                    l, g = layer_group(s)
                    if c == 0:
                        pe.wait_ge(s_nlo, KD * (U + 1))
                    pe.wait_ge(s_gelu, CF * U + c + 1)
                    for k in range(KD):
                        for p, (w, a) in enumerate(((w1_hi, nT_hi), (w1_hi, nT_lo), (w1_lo, nT_hi))):
                            mm = pe.matmul(HID[c % 2][:], w[:, l, k, c * P:(c + 1) * P], a[:, s % 2, k, :],
                                           start=(k == 0 and p == 0), stop=(k == KD - 1 and p == 2))
                    mm.then_inc(s_hid, 1)

                def output(U, s, c):
                    l, g = layer_group(s)
                    pe.wait_ge(s_split, CF * U + c + 1)
                    if c == 0:
                        pe.wait_ge(s_y, TG * U + TG)
                    for t in range(TG):
                        for p, (a, w) in enumerate(((hid_hi, w2_hi), (hid_hi, w2_lo), (hid_lo, w2_hi))):
                            mm = pe.matmul(FF[t // 2][:, (t % 2) * D:(t % 2 + 1) * D], a[:, c % RING, t * P:(t + 1) * P],
                                           w[:, l, c, :], start=(c == 0 and t % 2 == 0 and p == 0),
                                           stop=(c == CF - 1 and p == 2), skip_group_check=True)
                    mm.then_inc(s_ff, 1)

                def before():
                    spread(0, 0)
                    turn_attn(0, 0)
                    aggregate(0, 0)
                    spread(1, 1)
                    turn_n(0, 0)

                def lap(i, last):
                    for s in range(SLOTS):
                        U = i * SLOTS + s
                        nxt, nxt2 = not last or s + 1 < SLOTS, not last or s + 2 < SLOTS
                        for c in range(CF):
                            hidden(U, s, c)
                            if nxt and c == 0:
                                turn_attn(U + 1, s + 1)
                            if c >= 2:
                                output(U, s, c - 2)
                            if nxt and c == CF - 1:
                                turn_n(U + 1, s + 1)
                            if nxt and c == 2:
                                aggregate(U + 1, s + 1)
                            if nxt2 and c == 4:
                                spread(U + 2, s + 2)
                        output(U, s, CF - 2)
                        output(U, s, CF - 1)

                laps(pe, before, lap)

            @blk.scalar
            def _(act):
                act.sem_inc(s_gelu, 2)

                def gelu(U, s, c):
                    l, g = layer_group(s)
                    act.wait_ge(s_hid, CF * U + c + 1)
                    act.wait_ge(s_ff, CF * U + c + 1)
                    act.activation(hid[:, c % RING, :], HID[c % 2][:], ACT.Gelu, bias=b1_col[:, l, c:c + 1])
                    act.activation(hid_hi[:, c % RING, :], HID[c % 2][:], ACT.Gelu, bias=b1_col[:, l, c:c + 1]).then_inc(s_gelu, 1)

                def norm_y(U, par, ts):
                    for t in ts:
                        act.wait_ge(s_nmf, U + 1)
                        act.activation(y_tok[:, par, t, :], y_tok[:, par, t, :], ACT.Identity, bias=nm_f[:, t:t + 1],
                                       scale=rs_f[:, t:t + 1]).then_inc(s_yn, 1)

                def exp(V, s):
                    act.wait_ge(s_sh, V + 1)
                    at_least(act, s_atT, V)
                    for g in range(GPT):
                        act.activation(attn[g * N:(g + 1) * N, :, g * N:(g + 1) * N],
                                       shifted2[g * N:(g + 1) * N], ACT.Exp).then_inc(s_at, 1)

                def keep_attn(V, s):
                    act.wait_ge(s_atT, V + 1)
                    at_least(act, s_agg, V)
                    act.copy(attn_T[:].rearrange("p t i -> p (t i)"), ATT_T[:]).then_inc(s_atk, 1)

                def norm_n(V, s):
                    act.wait_ge(s_nma, V + 1)
                    for t in range(TG):
                        act.activation(n_tok[:, t, :], n_tok[:, t, :], ACT.Identity, bias=nm_a[:, t:t + 1],
                                       scale=rs_a[:, t:t + 1]).then_inc(s_n, 1)

                def split_n(V, s):
                    for k in range(KD):
                        act.wait_ge(s_nT, KD * V + k + 1)
                        act.copy(nT_hi[:, s % 2, k, :], NT_B[k][:]).then_inc(s_nhi, 1)

                def before():
                    act.wait_ge(s_zero, 1)
                    exp(0, 0)
                    keep_attn(0, 0)
                    norm_n(0, 0)
                    split_n(0, 0)
                    exp(1, 1)

                def lap(i, last):
                    for s in range(SLOTS):
                        U = i * SLOTS + s
                        nxt, nxt2 = not last or s + 1 < SLOTS, not last or s + 2 < SLOTS
                        for c in range(CF):
                            gelu(U, s, c)
                            if nxt and c == 0:
                                keep_attn(U + 1, s + 1)
                            if s > 0 and c in (2, 3):
                                norm_y(U - 1, (s - 1) % 2, range(2 * c - 4, 2 * c - 2))
                            if nxt and c == 6:
                                norm_n(U + 1, s + 1)
                            if nxt and c == CF - 1:
                                split_n(U + 1, s + 1)
                        if nxt2:
                            exp(U + 2, s + 2)
                    norm_y(i * SLOTS + SLOTS - 1, 1, range(TG))

                laps(act, before, lap)

            @blk.gpsimd
            def _(pool):
                pool.sem_inc(s_fin, 2)
                pool.sem_inc(s_x, 4)

                def rstd_of(dst, src, wait, count, done):
                    pool.wait_ge(wait, count)
                    pool.tensor_tensor(dst[:], src[:], minus_half[:], ALU.pow).then_inc(done, 1)

                def post(i, s, nxt):
                    l, g = layer_group(s)
                    U = i * SLOTS + s
                    pool.wait_ge(s_yn, TG * (U + 1))
                    y = y_tok[:, s % 2]
                    xg = x_cur[:, g] if l < L - 1 else y
                    pool.tensor_tensor(xg, y, g2_row[:, l].unsqueeze(1).broadcast_to([P, TG, D]), ALU.mult).then_inc(s_x, 1)
                    if nxt:
                        rstd_n(U + 2)
                    pool.wait_ge(s_x, 2 * U + 5)
                    pool.tensor_tensor(xg, xg, beta2_row[:, l].unsqueeze(1).broadcast_to([P, TG, D]), ALU.add).then_inc(s_x, 1)
                    if l == L - 1:
                        pool.wait_ge(s_x, 2 * U + 6)
                        pool.wait_ge(s_res[g % 2], 16 * (i * (QG // 2) + g // 2 + 1))
                        pool.tensor_tensor(x_fin[:, g % 2], x_fin[:, g % 2], y, ALU.add).then_inc(s_fin, 1)

                def make_base(V, s):
                    l, g = layer_group(s)
                    pool.wait_ge(s_n, TG * (V + 1))
                    pool.tensor_tensor(base[:, s % 2], n_tok[:], g1_row[:, l].unsqueeze(1).broadcast_to([P, TG, D]),
                                       ALU.mult).then_inc(s_base, 1)
                    pool.wait_ge(s_base, 2 * V + 1)
                    pool.tensor_tensor(base[:, s % 2], base[:, s % 2], c1_row[:, l].unsqueeze(1).broadcast_to([P, TG, D]),
                                       ALU.add).then_inc(s_base, 1)

                def rstd_n(V):
                    rstd_of(rs_a, ve_a, s_mva, (TG + 1) * (V + 1), s_rsa)

                def rstd_y(U):
                    rstd_of(rs_f, ve_f, s_mvf, (TG + 1) * (U + 1), s_rsf)

                def before():
                    rstd_n(0)
                    make_base(0, 0)

                def lap(i, last):
                    for s in range(SLOTS):
                        U, nxt = i * SLOTS + s, not last or s + 1 < SLOTS
                        if s > 0:
                            rstd_y(U - 1)
                            post(i, s - 1, nxt)
                        elif nxt:
                            rstd_n(U + 1)
                        if nxt:
                            make_base(U + 1, s + 1)
                    rstd_y(i * SLOTS + SLOTS - 1)
                    post(i, SLOTS - 1, False)

                laps(pool, before, lap)

            @blk.vector
            def _(dve):
                dve.memset(attn[:], 0.0).then_inc(s_zero, 1)
                dve.sem_inc(s_y, TG)
                score = Steps(dve, s_sc, 7)

                def split(U, c):
                    dve.wait_ge(s_gelu, CF * U + c + 3)
                    dve.tensor_tensor(hid_lo[:, c % RING, :], hid[:, c % RING, :], hid_hi[:, c % RING, :].bitcast(F32),
                                      ALU.subtract).then_inc(s_split, 1)

                def take_y(i, s):
                    U = i * SLOTS + s
                    dve.wait_ge(s_ff, CF * (U + 1) + RING)
                    dve.wait_ge(s_base, 2 * U + 2)
                    dve.wait_ge(s_x, 2 * U + 2)
                    if 0 <= s - 2 - (L - 1) * QG:
                        dve.wait_ge(s_fin, i * QG + s + 1 - (L - 1) * QG)
                    elif s < 2:
                        dve.wait_ge(s_fin, i * QG + s + 1)
                    for t in range(TG):
                        dve.tensor_tensor(y_tok[:, s % 2, t, :], FF[t // 2][:, (t % 2) * D:(t % 2 + 1) * D], base[:, s % 2, t, :],
                                          ALU.add).then_inc(s_y, 1)

                def stats_y(U, s):
                    for t in range(TG):
                        dve.wait_ge(s_y, TG * (U + 1) + t + 1)
                        dve.bn_stats(st_f[:, t, :], y_tok[:, s % 2, t, :]).then_inc(s_stf, 1)
                    pause(dve, s_stf, TG * U + TG, s_own)
                    for t in range(TG):
                        dve.bn_aggr(mv_f[:, t, :], st_f[:, t, :]).then_inc(s_mvf, 1)
                    dve.wait_ge(s_mvf, (TG + 1) * U + TG)
                    dve.tensor_scalar(ve_f[:].unsqueeze(2), mv_f[:, :, 1:2], EPS, None, ALU.add).then_inc(s_mvf, 1)

                def shift_y(U, s):
                    dve.wait_ge(s_rsf, U + 1)
                    dve.scalar_tensor_tensor(nm_f[:].unsqueeze(2), mv_f[:, :, 0:1], -1.0, rs_f[:].unsqueeze(2),
                                             ALU.mult, ALU.mult).then_inc(s_nmf, 1)

                def dots_of(i, s, ts):
                    l, g = layer_group(s)
                    V = i * SLOTS + s
                    if ts[0] == 0:
                        if l == 0:
                            dve.wait_ge(s_in[g], 32 * (i + s // SLOTS + 1))
                        else:
                            dve.wait_ge(s_x, 2 * (V - QG) + 6)
                    for t in ts:
                        for j, dst in enumerate((s_src, s_dst)):
                            n = 2 * t + j
                            at_least(dve, s_dots, 8 * V + n)
                            dve.tensor_tensor_reduce(dots[:], x_cur[:, g, t, :], att_row[:, l, j, :], 1.0, 0.0,
                                                     ALU.mult, ALU.add, dst[:, t:t + 1]).then_inc(s_dots, 1)

                def diagonal(i, s):
                    l, g = layer_group(s)
                    V = i * SLOTS + s
                    dve.wait_ge(s_dots, 2 * TG * (V + 1))
                    at_least(dve, s_spread, V)
                    dve.tensor_tensor(diag2[:], node_of[:].unsqueeze(1).broadcast_to([P, TG, N]),
                                      s_dst[:].unsqueeze(2).broadcast_to([P, TG, N]), ALU.mult).then_inc(s_dg, 1)
                    score.unit(V)
                    score.done(dve.tensor_scalar(src_b[:], s_src[:], attb_row[:, l:l + 1], None, ALU.add))
                    if l == 0:
                        score.done(dve.tensor_tensor(mask_sum[:], adj_raw[:, g], node_of[:].unsqueeze(1).broadcast_to([P, TG, N]),
                                                     ALU.add))
                        score.wait()
                        score.done(dve.tensor_scalar(mask[:, g], mask_sum[:], 0.0, NEG, ALU.is_le, ALU.mult))
                        score.wait()
                    else:
                        score.k += 2
                        dve.sem_inc(s_sc, 2)

                def scores(i, s):
                    l, g = layer_group(s)
                    V = i * SLOTS + s
                    score.wait()
                    dve.wait_ge(s_spread, V + 1)
                    score.done(dve.tensor_tensor(masked2[:], SPREAD[:, 0:TG * N].rearrange("p (t j) -> p t j", t=TG), mask[:, g],
                                                 ALU.add))
                    score.wait()
                    score.done(dve.tensor_reduce(top2[:], masked2[:], AX, ALU.max))
                    dve.tensor_tensor(scored2[:], masked2[:], src_b[:].unsqueeze(2).broadcast_to([P, TG, N]),
                                      ALU.add).then_inc(s_scd, 1)
                    score.wait()
                    score.done(dve.tensor_tensor(top2_s[:], top2[:], src_b[:], ALU.add))
                    dve.wait_ge(s_scd, 2 * V + 1)
                    dve.scalar_tensor_tensor(leaky2[:], scored2[:], SLOPE, scored2[:], ALU.mult, ALU.max).then_inc(s_scd, 1)
                    score.wait()
                    score.done(dve.scalar_tensor_tensor(top2_l[:], top2_s[:], SLOPE, top2_s[:], ALU.mult, ALU.max))
                    score.wait()
                    dve.wait_ge(s_scd, 2 * V + 2)
                    at_least(dve, s_at, GPT * V)
                    dve.tensor_tensor(shifted2[:], leaky2[:], top2_l[:].unsqueeze(2).broadcast_to([P, TG, N]),
                                      ALU.subtract).then_inc(s_sh, 1)

                def sums(V):
                    dve.wait_ge(s_at, GPT * (V + 1))
                    dve.tensor_reduce(row_sum[:], attn[:], AX, ALU.add).then_inc(s_inv, 1)
                    dve.wait_ge(s_inv, 2 * V + 1)
                    dve.reciprocal(row_inv[:], row_sum[:]).then_inc(s_inv, 1)

                def residual(i, s):
                    l, g = layer_group(s)
                    V = i * SLOTS + s
                    dve.wait_ge(s_agg, V + 1)
                    dve.wait_ge(s_inv, 2 * V + 2)
                    at_least(dve, s_nT, KD * V)
                    at_least(dve, s_base, 2 * V - 1)
                    for t in range(TG):
                        dve.scalar_tensor_tensor(n_tok[:, t, :], AGG[t // 2][:, (t % 2) * D:(t % 2 + 1) * D], row_inv[:, t:t + 1],
                                                 x_cur[:, g, t, :], ALU.mult, ALU.add).then_inc(s_u, 1)

                def stats_n(V):
                    for t in range(TG):
                        dve.wait_ge(s_u, TG * V + t + 1)
                        dve.bn_stats(st_a[:, t, :], n_tok[:, t, :]).then_inc(s_sta, 1)
                    pause(dve, s_sta, TG * V + TG, s_own)
                    for t in range(TG):
                        dve.bn_aggr(mv_a[:, t, :], st_a[:, t, :]).then_inc(s_mva, 1)
                    dve.wait_ge(s_mva, (TG + 1) * V + TG)
                    dve.tensor_scalar(ve_a[:].unsqueeze(2), mv_a[:, :, 1:2], EPS, None, ALU.add).then_inc(s_mva, 1)

                def shift_n(V):
                    dve.wait_ge(s_rsa, V + 1)
                    dve.scalar_tensor_tensor(nm_a[:].unsqueeze(2), mv_a[:, :, 0:1], -1.0, rs_a[:].unsqueeze(2),
                                             ALU.mult, ALU.mult).then_inc(s_nma, 1)

                def split_n(V, s):
                    for k in range(KD):
                        dve.wait_ge(s_nhi, KD * V + k + 1)
                        dve.tensor_tensor(nT_lo[:, s % 2, k, :], NT_B[k][:], nT_hi[:, s % 2, k, :].bitcast(F32),
                                          ALU.subtract).then_inc(s_nlo, 1)

                def before():
                    for V in range(2):
                        dots_of(0, V, range(TG))
                        diagonal(0, V)
                        scores(0, V)
                        if V == 0:
                            sums(0)
                            residual(0, 0)
                            stats_n(0)
                            shift_n(0)
                    split_n(0, 0)

                def lap(i, last):
                    for s in range(SLOTS):
                        U = i * SLOTS + s
                        nxt, nxt2 = not last or s + 1 < SLOTS, not last or s + 2 < SLOTS
                        if s > 0:
                            take_y(i, s - 1)
                        if nxt2:
                            dots_of(i, s + 2, range(0, 2))
                        split(U, 0)
                        if s > 0:
                            stats_y(U - 1, s - 1)
                        split(U, 1)
                        if s > 0:
                            shift_y(U - 1, s - 1)
                        if nxt2:
                            dots_of(i, s + 2, range(2, 4))
                            diagonal(i, s + 2)
                        split(U, 2)
                        if nxt:
                            sums(U + 1)
                            residual(i, s + 1)
                        split(U, 3)
                        if nxt:
                            stats_n(U + 1)
                        split(U, 4)
                        if nxt:
                            shift_n(U + 1)
                        if nxt2:
                            scores(i, s + 2)
                        split(U, 5)
                        split(U, 6)
                        split(U, 7)
                        if nxt:
                            split_n(U + 1, s + 1)
                    take_y(i, SLOTS - 1)
                    stats_y(i * SLOTS + SLOTS - 1, SLOTS - 1)
                    shift_y(i * SLOTS + SLOTS - 1, SLOTS - 1)

                laps(dve, before, lap)

_INS = ['x', 'adj', 'L0_gnn_W_proj', 'L0_gnn_W_att', 'L0_gnn_b_att', 'L1_gnn_attn_w', 'L1_gnn_attn_b', 'L1_gnn_W1',
        'L1_gnn_b1', 'L1_gnn_W2', 'L1_gnn_b2', 'L1_gnn_g1', 'L1_gnn_beta1', 'L1_gnn_g2', 'L1_gnn_beta2']
_OUTS = [((128, 64, 256), 'float32')]


def kernel(**inputs):
    import numpy as _np
    import concourse.bacc as _bacc
    from concourse import mybir as _mybir
    from concourse.bass_utils import run_bass_kernel_spmd as _run

    nc = _bacc.Bacc("TRN2", target_bir_lowering=False, num_devices=1)
    arrays, args = {}, []
    for name in _INS:
        a = _np.ascontiguousarray(inputs[name])
        arrays[f"in_{name}_dram"] = a
        args.append(nc.dram_tensor(f"in_{name}_dram", a.shape, _mybir.dt.from_np(a.dtype), kind="ExternalInput").ap())
    for i, (shape, dtype) in enumerate(_OUTS):
        dt = _mybir.dt.from_np(_np.dtype(dtype))
        args.append(nc.dram_tensor(f"out_{i}_dram", shape, dt, kind="ExternalOutput").ap())
    graph_net(nc, *args)
    r = _run(nc, [arrays], core_ids=[0])
    got = tuple(r.results[0][f"out_{i}_dram"] for i in range(len(_OUTS)))
    return got[0]
```

```python
from contextlib import ExitStack

import concourse.bass as bass
from concourse import mybir

F32 = mybir.dt.float32
F32R = mybir.dt.float32r
I32 = mybir.dt.int32
ALU = mybir.AluOpType
ACT = mybir.ActivationFunctionType
AX = mybir.AxisListType.X

P = 128
NEG = -1e30
SLOPE = 0.2
EPS = 1e-5


def at_least(eng, sem, value):
    if not isinstance(value, int) or value > 0:
        eng.wait_ge(sem, value)


def pause(eng, sem, value, own):
    if not isinstance(value, int) or value > 0:
        eng.wait_ge(sem, value)
        eng.sem_inc(own, 1)


class Steps:

    def __init__(self, eng, sem, per):
        self.eng, self.sem, self.per, self.base, self.k = eng, sem, per, 0, 0

    def unit(self, n):
        assert self.k in (0, self.per), self.k
        self.base, self.k = n * self.per, 0

    def done(self, instruction):
        self.k += 1
        instruction.then_inc(self.sem, 1)

    def wait(self):
        self.eng.wait_ge(self.sem, self.base + self.k)


def graph_net(nc, x, adj, w_proj, w_att, b_att, attn_w, attn_b, w1, b1, w2, b2, g1, beta1, g2, beta2, out):
    B, N, D = x.shape
    H, K2 = w_att.shape
    HK = K2 // 2
    L, _, F = w1.shape
    NT = B * N // P
    GPT = P // N
    KD = D // P
    CF = F // P
    TG = 4
    NG = NT // TG
    TOK = TG * P
    QG = 4
    LAPS = NG // QG
    SLOTS = L * QG
    WC = D + 2 * H
    HC = HK + 1
    RING = 2

    x_v = x.rearrange("(t g) n d -> (g n) t d", g=GPT)
    out_v = out.rearrange("(t g) n d -> (g n) t d", g=GPT)
    adj_v = adj.rearrange("(t g) i j -> (g i) t j", g=GPT)
    res_d = nc.dram_tensor("first_block_out", (P, NT, D), F32, kind="Internal").ap()
    act_d = nc.dram_tensor("second_block_in", (P, NT, D), F32, kind="Internal").ap()

    def row(ap, n):
        return ap.rearrange("(a n) -> a n", a=1).broadcast_to([P, n])

    ctx = ExitStack()
    with ctx:
        def sb(name, shape, dt=F32, where=None):
            return (where or ctx).enter_context(nc.sbuf_tensor(name, shape, dt))

        def sem(name):
            return ctx.enter_context(nc.semaphore(name))

        bank = [ctx.enter_context(nc.psum_tensor(f"bank{i}", [P, 512], F32)) for i in range(8)]

        ident = sb("ident", [P, P])
        node_of = sb("node_of", [P, N])
        same_graph = sb("same_graph", [P, P])
        minus_half = sb("minus_half", [P, TG])
        w1_hi, w1_lo = (sb(n, [P, L, KD, F], F32R) for n in ("w1_hi", "w1_lo"))
        w2_hi, w2_lo = (sb(n, [P, L, CF, D], F32R) for n in ("w2_hi", "w2_lo"))
        b1_col = sb("b1_col", [P, L, CF])
        g1_row = sb("g1_row", [P, L, D])
        att_row = sb("att_row", [P, L, 2, D])
        attb_row = sb("attb_row", [P, L])

        first = ExitStack()
        with first:
            wcat_hi, wcat_lo = (sb(n, [P, KD, WC], F32R, where=first) for n in ("wcat_hi", "wcat_lo"))
            batt_row = sb("batt_row", [P, H], where=first)
            b1_raw = sb("b1_raw", [P, L, CF], where=first)
            g1_col, beta1_col = (sb(n, [P, L, KD], where=first) for n in ("g1_col", "beta1_col"))
            raw = sb("raw_weights", [P, L, KD * F], where=first)
            s_w1 = [sem(f"w1_loaded{l}") for l in range(L)]
            s_w2, s_ready = sem("w2_loaded"), sem("w2_seen")
            s_col, s_rows, s_cat, s_batt = sem("columns_loaded"), sem("rows_loaded"), sem("wcat_loaded"), sem("batt_loaded")
            s_fill, s_const, s_same = sem("consts_filled"), sem("consts_made"), sem("same_graph_made")
            s_su, s_cathi, s_catlo = sem("wcat_steps"), sem("wcat_hi_made"), sem("wcat_lo_made")
            s_bias, s_b1 = sem("bias_products"), sem("bias_kept")
            s_whi, s_wlo, s_w2lo = sem("weight_hi"), sem("w1_lo_made"), sem("w2_lo_made")
            W1P, W2P = KD * F // 4, L * CF * D // (NT - 16)
            XR = 16
            xin = sb("xin", [P, XR, D], where=first)
            adjin = sb("adjin", [P, XR, N], I32, where=first)
            hrelu = sb("hrelu", [P, 2, D], where=first)
            hT_hi, hT_lo = (sb(n, [P, 2, D], F32R, where=first) for n in ("hT_hi", "hT_lo"))
            xh = sb("xh", [P, 4, H, HC], where=first)
            a_src = sb("a_src", [P, 4, H], where=first)
            a_dst = sb("a_dst", [P, 4, H], where=first)
            dst_diag = sb("dst_diag", [P, 2, H, N], where=first)
            no_edge = sb("no_edge", [P, N], where=first)
            masked, scored, leaky, shifted = (sb(n, [P, H, N], where=first) for n in ("masked", "scored", "leaky", "shifted"))
            top, top_s, top_l = (sb(n, [P, H], where=first) for n in ("top", "top_s", "top_l"))
            weights = sb("weights", [P, H, P], where=first)
            weights_T = sb("weights_T", [P, 2, H, P], where=first)
            inv = sb("inv", [P, H], where=first)
            headout = sb("headout", [P, D], where=first)
            x_res = sb("x_res", [P, 8, D], where=first)
            x_act = sb("x_act", [P, 8, D], where=first)
            scratch = x_act[:].rearrange("p a d -> p (a d)")
            wcat = scratch[:, 0:KD * WC].rearrange("p (k w) -> p k w", k=KD)
            watt_row = scratch[:, KD * WC:KD * WC + 2 * D].rearrange("p (i h k) -> p i h k", i=2, h=H)
            prod = scratch[:, KD * WC + 2 * D:KD * WC + 3 * D].rearrange("p (h k) -> p h k", h=H)
            stats = sb("stats", [P, 2, 6], where=first)
            mv = sb("mv", [P, 4, 2, 2], where=first)
            vare, rstd, nmr = (sb(n, [P, 4, 2], where=first) for n in ("vare", "rstd", "nmr"))

            q_own, q_own_sp, q_ld, q_ne = sem("q_paused"), sem("q_sync_paused"), sem("tiles_loaded"), sem("q_no_edge")
            q_s0, q_s1, q_vs, q_vh = sem("q_stats_in"), sem("q_stats_result"), sem("q_score_steps"), sem("q_heads_steps")
            q_st = sem("first_stored")
            q_zero = sem("first_filled")
            q_mv, q_rs, q_nmr, q_h = sem("q_mean_var"), sem("q_rstd"), sem("q_shift"), sem("q_h")
            q_tr, q_hi, q_lo = sem("q_hT"), sem("q_hT_hi"), sem("q_hT_lo")
            q_xp, q_xh, q_asd, q_diag = sem("q_proj"), sem("q_xh"), sem("q_src_dst"), sem("q_diag")
            q_bc, q_msk, q_sc, q_d, q_e = sem("q_dst_spread"), sem("q_masked"), sem("q_scored"), sem("q_shifted"), sem("q_weights")
            q_wt, q_ev, q_ag = sem("q_weights_T"), sem("q_weights_T_kept"), sem("q_heads")
            q_res, q_mean, q_act = sem("q_res"), sem("q_mean"), sem("q_act")
            blk = first.enter_context(nc.Block())

            HEAD, LAG = 16, 10
            FIRST_PART = 2
            assert W2P * (NT - HEAD) == L * CF * D

            def steps(eng, step):
                for tau in range(HEAD):
                    step(tau, tau)
                with eng.Fori(HEAD // 4, NT // 4) as i:
                    for t in range(4):
                        step(i * 4 + t, t)
                for tau in range(NT, NT + LAG):
                    step(tau, tau)

            def has(T):
                return not isinstance(T, int) or 0 <= T < NT

            def splits_w1(tau):
                return isinstance(tau, int) and FIRST_PART <= tau < FIRST_PART + 4 * L

            def splits_w2(tau):
                return not isinstance(tau, int)

            def raw_part(tau):
                return raw[:].rearrange("p l f -> p (l f)").rearrange("p (n d) -> p n d", d=W2P)[:, tau - HEAD, :]

            def w2_part(w, tau):
                return w.rearrange("p l c d -> p (l c d)").rearrange("p (n d) -> p n d", d=W2P)[:, tau - HEAD, :]

            def counted(S):
                return not isinstance(S, int) or 0 <= S < NT + 9

            @blk.sync
            def _(sp):
                def load_group(g, part):
                    pause(sp, q_ld, 32 * g, q_own_sp)
                    sp.dma_start(xin[:, part * 4:part * 4 + 4, :], x_v[:, bass.ts(g, 4), :]).then_inc(q_ld, 16)
                    sp.dma_start(adjin[:, part * 4:part * 4 + 4, :], adj_v[:, bass.ts(g, 4), :]).then_inc(q_ld, 16)

                def store_group(g, half):
                    pause(sp, q_res, 4 * g + 4, q_own_sp)
                    pause(sp, q_act, 4 * g + 4, q_own_sp)
                    pause(sp, q_st, 32 * g, q_own_sp)
                    sp.dma_start(res_d[:, bass.ts(g, 4), :], x_res[:, half * 4:half * 4 + 4, :]).then_inc(q_st, 16)
                    sp.dma_start(act_d[:, bass.ts(g, 4), :], x_act[:, half * 4:half * 4 + 4, :]).then_inc(q_st, 16)

                with nc.allow_non_contiguous_dma(reason="small columns, broadcast rows"):
                    for k in range(KD):
                        sp.dma_start(wcat[:, k, 0:D], w_proj[k * P:(k + 1) * P, :]).then_inc(s_cat, 16)
                    for i in range(2):
                        sp.dma_start(watt_row[:, i], w_att[:, i * HK:(i + 1) * HK].rearrange("(a h) k -> a h k", a=1)
                                     .broadcast_to([P, H, HK])).then_inc(s_cat, 16)
                    sp.dma_start(beta1_col[:], beta1.rearrange("l (c p) -> p l c", p=P)).then_inc(s_col, 16)
                    sp.dma_start(b1_raw[:], b1.rearrange("l (c p) -> p l c", p=P)).then_inc(s_col, 16)
                    sp.dma_start(g1_col[:], g1.rearrange("l (c p) -> p l c", p=P)).then_inc(s_col, 16)
                    load_group(0, 0)
                    sp.dma_start(batt_row[:], row(b_att, H)).then_inc(s_batt, 16)
                    for g in range(1, 4):
                        load_group(g, g)
                    sp.dma_start(g1_row[:].rearrange("p l d -> p (l d)"),
                                 row(g1.rearrange("l d -> (l d)"), L * D)).then_inc(s_rows, 16)
                    sp.dma_start(att_row[:].rearrange("p l a d -> p (l a d)"),
                                 row(attn_w.rearrange("l d -> (l d)"), L * 2 * D)).then_inc(s_rows, 16)
                    sp.dma_start(attb_row[:], row(attn_b, L)).then_inc(s_rows, 16)
                with sp.Fori(0, NG // 4 - 1) as i:
                    for part in range(4):
                        pause(sp, q_res, i * 16 + (part * 4 + 4), q_own_sp)
                        load_group(i * 4 + (part + 4), part)
                        store_group(i * 4 + part, part % 2)
                for g in range(NG - 4, NG):
                    store_group(g, g % 2)
                sp.wait_ge(q_st, 32 * NG)

            @blk.tensor
            def _(pe):
                def step(tau, t):
                    if isinstance(tau, int) and tau < 2 * L:
                        l, half = tau // 2, tau % 2
                        if tau == 0:
                            pe.wait_ge(s_col, 48)
                        pe.wait_ge(s_w1[l], 16)
                        for c in range(half * CF // 2, (half + 1) * CF // 2):
                            for k in range(KD):
                                mm = pe.matmul(bank[7][:, H * HC + l * CF + c:H * HC + l * CF + c + 1],
                                               raw[:, l, k * F + c * P:k * F + (c + 1) * P], beta1_col[:, l, k:k + 1],
                                               start=(k == 0), stop=(k == KD - 1))
                        mm.then_inc(s_bias, 1)
                    T, r = tau - 6, (t - 6)
                    if has(T):
                        if isinstance(T, int) and T == 0:
                            pe.wait_ge(s_same, GPT + 1)
                        pe.wait_ge(q_diag, T + 1)
                        at_least(pe, q_msk, T)
                        pe.matmul(bank[4][:], same_graph[:], dst_diag[:, r % 2].rearrange("p h j -> p (h j)"),
                                  start=True, stop=True).then_inc(q_bc, 1)
                    T, r = tau - 2, (t - 2)
                    if has(T):
                        if isinstance(T, int) and T == 0:
                            pe.wait_ge(s_const, 2)
                        pe.wait_ge(q_h, T + 1)
                        at_least(pe, q_lo, T - 1)
                        for k in range(KD):
                            mm = pe.transpose(bank[r % 2][:, k * P:(k + 1) * P], hrelu[:, r % 2, k * P:(k + 1) * P], ident[:])
                        mm.then_inc(q_tr, 1)
                    T, r = tau - 8, (t - 8)
                    if has(T):
                        pe.wait_ge(q_ev, 2 * T + 2)
                        pe.wait_ge(q_xh, T + 1)
                        at_least(pe, q_vh, 2 * T)
                        if isinstance(T, int) and T == 0:
                            pe.wait_ge(s_b1, 1)
                        for h in range(H):
                            mm = pe.matmul(bank[7][:, h * HC:(h + 1) * HC], weights_T[:, r % 2, h, :],
                                           xh[:, r % 4, h, :], start=True, stop=True)
                        mm.then_inc(q_ag, 1)
                    T, r = tau - 7, (t - 7)
                    if has(T):
                        pe.wait_ge(q_e, 2 * T + 2)
                        at_least(pe, q_ev, 2 * T)
                        for h in range(H):
                            mm = pe.transpose(bank[5 + h // 4][:, (h % 4) * P:(h % 4 + 1) * P], weights[:, h, :], ident[:])
                        mm.then_inc(q_wt, 1)
                    T, r = tau - 3, (t - 3)
                    if has(T):
                        if isinstance(T, int) and T == 0:
                            pe.wait_ge(s_cathi, 1)
                            pe.wait_ge(s_catlo, 1)
                        pe.wait_ge(q_lo, T + 1)
                        at_least(pe, q_xh, T - 1)
                        at_least(pe, q_asd, 2 * (T - 1))
                        for k in range(KD):
                            for p, (a, w) in enumerate(((hT_hi, wcat_hi), (hT_hi, wcat_lo), (hT_lo, wcat_hi))):
                                mm = pe.matmul(bank[2 + r % 2][:, 0:WC], a[:, r % 2, k * P:(k + 1) * P], w[:, k, :],
                                               start=(k == 0 and p == 0), stop=(k == KD - 1 and p == 2))
                        mm.then_inc(q_xp, 1)

                steps(pe, step)

            @blk.scalar
            def _(act):
                act.wait_ge(s_cat, 16 * (KD + 2))
                for l in range(L):
                    act.dma_start(raw[:, l].rearrange("p (c f) -> p c f", c=KD),
                                  w1[l].rearrange("(c p) f -> p c f", p=P)).then_inc(s_w1[l], 16)
                act.wait_ge(s_su, 2 * KD * 2)
                act.copy(wcat_hi[:], wcat[:]).then_inc(s_cathi, 1)

                def step(tau, t):
                    w1_part = tau - FIRST_PART
                    if splits_w1(tau):
                        l, q = w1_part // 4, w1_part % 4
                        if w1_part == 0:
                            act.wait_ge(s_col, 48)
                        act.wait_ge(s_bias, 2 * (l + 1))
                        act.activation(w1_hi[:, l].rearrange("p c f -> p (c f)")[:, q * W1P:(q + 1) * W1P],
                                       raw[:, l, q * W1P:(q + 1) * W1P], ACT.Copy,
                                       scale=g1_col[:, l, q // 2:q // 2 + 1]).then_inc(s_whi, 1)
                    if splits_w2(tau):
                        act.copy(w2_part(w2_hi, tau), raw_part(tau)).then_inc(s_whi, 1)
                    T, r = tau - 2, (t - 2)
                    if has(T):
                        act.wait_ge(q_tr, T + 1)
                        at_least(act, q_xp, T - 1)
                        act.copy(hT_hi[:, r % 2, :], bank[r % 2][:, 0:D]).then_inc(q_hi, 1)
                    T, r = tau - 1, (t - 1)
                    if has(T):
                        act.wait_ge(q_nmr, T + 1)
                        at_least(act, q_tr, T - 1)
                        act.activation(hrelu[:, r % 2, :], xin[:, T % XR, :], ACT.Relu,
                                       bias=nmr[:, r % 4, 0:1], scale=rstd[:, r % 4, 0:1]).then_inc(q_h, 1)
                    T, r = tau - 4, (t - 4)
                    if has(T):
                        act.wait_ge(q_xp, T + 1)
                        at_least(act, q_ag, T - 3)
                        if isinstance(T, int) and T == 0:
                            act.wait_ge(q_zero, 2)
                        act.copy(xh[:, r % 4, :, 0:HK], bank[2 + r % 2][:, 0:D].rearrange("p (h k) -> p h k", h=H)).then_inc(q_xh, 1)
                    T, r = tau - 7, (t - 7)
                    if has(T):
                        act.wait_ge(q_wt, T + 1)
                        at_least(act, q_ag, T - 1)
                        for b in range(2):
                            act.copy(weights_T[:, r % 2, 4 * b:4 * b + 4, :].rearrange("p h i -> p (h i)"),
                                     bank[5 + b][:]).then_inc(q_ev, 1)
                    T, r = tau - 10, (t - 10)
                    if has(T):
                        act.wait_ge(q_nmr, T + 10)
                        if r % 4 == 0:
                            at_least(act, q_st, 8 * (T - 4))
                        act.activation(x_act[:, T % 8, :],
                                       x_res[:, T % 8, :], ACT.Relu,
                                       bias=nmr[:, (r + 1) % 4, 1:2], scale=rstd[:, (r + 1) % 4, 1:2]).then_inc(q_act, 1)
                    T, r = tau - 6, (t - 6)
                    if has(T):
                        act.wait_ge(q_d, T + 1)
                        at_least(act, q_wt, T)
                        if isinstance(T, int) and T == 0:
                            act.wait_ge(q_zero, 1)
                        for g in range(GPT):
                            act.activation(weights[g * N:(g + 1) * N, :, g * N:(g + 1) * N],
                                           shifted[g * N:(g + 1) * N], ACT.Exp).then_inc(q_e, 1)
                    if isinstance(tau, int) and tau == HEAD - 1:
                        act.wait_ge(s_w2, 16 * L)
                        act.sem_inc(s_ready, 1)

                steps(act, step)

            @blk.gpsimd
            def _(pool):
                pool.memset(ident[:], 0.0).then_inc(s_fill, 1)
                pool.memset(node_of[:], 0.0).then_inc(s_fill, 1)
                pool.memset(minus_half[:], -0.5).then_inc(s_const, 1)
                pool.wait_ge(s_fill, 2)
                pool.affine_select(out=ident[:], in_=ident[:], compare_op=ALU.not_equal, fill=1.0, base=0,
                                   pattern=[[-1, P]], channel_multiplier=1).then_inc(s_const, 1)
                pool.affine_select(out=node_of[:], in_=node_of[:], compare_op=ALU.not_equal, fill=1.0, base=0,
                                   pattern=[[-1, N]], channel_multiplier=1).then_inc(s_fill, 1)
                pool.wait_ge(s_fill, 3)
                pool.affine_select(out=node_of[:], in_=node_of[:], compare_op=ALU.not_equal, fill=1.0, base=-N,
                                   pattern=[[-1, N]], channel_multiplier=1).then_inc(s_const, 1)
                pool.wait_ge(s_const, 3)

                def step(tau, t):
                    S, r = tau - 1, (t - 1)
                    if counted(S):
                        pool.wait_ge(q_mv, S + 1)
                        at_least(pool, q_act, S - 12)
                        pool.tensor_tensor(rstd[:, r % 4, :], vare[:, r % 4, :], minus_half[:, 0:2], ALU.pow).then_inc(q_rs, 1)
                    T, r = tau - 6, (t - 6)
                    if has(T):
                        pool.wait_ge(q_msk, T + 1)
                        at_least(pool, q_d, T)
                        pool.tensor_tensor(scored[:], masked[:], a_src[:, r % 4, :].unsqueeze(2).broadcast_to([P, H, N]),
                                           ALU.add).then_inc(q_sc, 1)
                    if splits_w2(tau):
                        pool.wait_ge(s_whi, 4 * L + 1 + (tau - HEAD))
                        pool.tensor_tensor(w2_part(w2_lo, tau), raw_part(tau),
                                           w2_part(w2_hi, tau).bitcast(F32), ALU.subtract).then_inc(s_w2lo, 1)
                    if splits_w1(tau) and (tau - FIRST_PART) % 4 == 3:
                        l = (tau - FIRST_PART) // 4
                        pool.wait_ge(s_wlo, 4 * (l + 1))
                        pool.dma_start(raw[:, l].rearrange("p (c d) -> p c d", c=CF),
                                       w2[l].rearrange("(c p) d -> p c d", p=P)).then_inc(s_w2, 16)
                    T, r = tau - 4, (t - 4)
                    if has(T):
                        pool.wait_ge(q_asd, 2 * T + 2)
                        at_least(pool, q_bc, T - 1)
                        pool.tensor_tensor(dst_diag[:, r % 2], node_of[:].unsqueeze(1).broadcast_to([P, H, N]),
                                           a_dst[:, r % 4, :].unsqueeze(2).broadcast_to([P, H, N]), ALU.mult).then_inc(q_diag, 1)
                    T, r = tau - 8, (t - 8)
                    if has(T):
                        pool.wait_ge(q_vh, 2 * T + 2)
                        if r % 4 == 0:
                            at_least(pool, q_st, 8 * (T - 4))
                        pool.tensor_tensor(x_res[:, T % 8, :], headout[:], xin[:, T % XR, :], ALU.add).then_inc(q_res, 1)

                steps(pool, step)
                pool.wait_ge(s_w2lo, NT - HEAD)
                pool.wait_ge(s_rows, 16 * 3)

            @blk.vector
            def _(dve):
                dve.memset(same_graph[:], 0.0).then_inc(s_same, 1)
                dve.wait_ge(s_same, 1)
                for g in range(GPT):
                    dve.memset(same_graph[g * N:(g + 1) * N, g * N:(g + 1) * N], 1.0).then_inc(s_same, 1)
                dve.wait_ge(s_cat, 16 * (KD + 2))
                done = 0
                for k in range(KD):
                    for i in range(2):
                        if done:
                            dve.wait_ge(s_su, done)
                        dve.tensor_tensor(prod[:], wcat[:, k, 0:D].rearrange("p (h k) -> p h k", h=H), watt_row[:, i],
                                          ALU.mult).then_inc(s_su, 1)
                        dve.wait_ge(s_su, done + 1)
                        dve.tensor_reduce(wcat[:, k, D + i * H:D + (i + 1) * H], prod[:], AX, ALU.add).then_inc(s_su, 1)
                        done += 2
                dve.wait_ge(s_cathi, 1)
                dve.tensor_tensor(wcat_lo[:], wcat[:], wcat_hi[:].bitcast(F32), ALU.subtract).then_inc(s_catlo, 1)
                dve.memset(weights[:], 0.0).then_inc(q_zero, 1)
                dve.memset(xh[:, :, :, HK:HC], 1.0).then_inc(q_zero, 1)
                dve.memset(mv[:], 0.0).then_inc(q_zero, 1)
                dve.wait_ge(q_zero, 3)
                score = Steps(dve, q_vs, 4)
                heads = Steps(dve, q_vh, 2)

                def step(tau, t):
                    scores = tau - 6
                    if has(scores):
                        dve.wait_ge(q_ne, scores + 1)
                        dve.wait_ge(q_bc, scores + 1)
                        at_least(dve, q_sc, scores)
                        dve.tensor_tensor(masked[:], bank[4][:].rearrange("p (h j) -> p h j", h=H),
                                          no_edge[:].unsqueeze(1).broadcast_to([P, H, N]), ALU.add).then_inc(q_msk, 1)
                    S, s = tau - 1, (t - 1)
                    if counted(S):
                        dve.wait_ge(q_mean, S + 1)
                        dve.tensor_scalar(vare[:, s % 4].unsqueeze(2), mv[:, s % 4, :, 1:2], EPS, None, ALU.add).then_inc(q_mv, 1)
                    if has(tau):
                        if t % 4 == 0:
                            pause(dve, q_ld, 32 * (tau // 4 + 1), q_own)
                        dve.bn_stats(stats[:, 0, :], xin[:, tau % XR, :]).then_inc(q_s0, 1)
                    if has(scores):
                        score.unit(scores)
                        dve.wait_ge(q_msk, scores + 1)
                        score.done(dve.tensor_reduce(top[:], masked[:], AX, ALU.max))
                    T, r = tau - 3, (t - 3)
                    if has(T):
                        dve.wait_ge(q_hi, T + 1)
                        at_least(dve, q_xp, T - 1)
                        dve.tensor_tensor(hT_lo[:, r % 2, :], bank[r % 2][:, 0:D], hT_hi[:, r % 2, :].bitcast(F32),
                                          ALU.subtract).then_inc(q_lo, 1)
                    if isinstance(tau, int) and tau == 2 * L:
                        dve.wait_ge(s_bias, 2 * L)
                        dve.tensor_tensor(b1_col[:].rearrange("p l c -> p (l c)"), bank[7][:, H * HC:H * HC + L * CF],
                                          b1_raw[:].rearrange("p l c -> p (l c)"), ALU.add).then_inc(s_b1, 1)
                    T = tau - 8
                    if has(T):
                        heads.unit(T)
                        dve.wait_ge(q_ag, T + 1)
                        G = bank[7][:, 0:H * HC].rearrange("p (h k) -> p h k", h=H)
                        heads.done(dve.reciprocal(inv[:].unsqueeze(2), G[:, :, HK:HC]))
                    if has(scores):
                        score.wait()
                        score.done(dve.tensor_tensor(top_s[:], top[:], a_src[:, (t - 6) % 4, :], ALU.add))
                    if counted(S):
                        dve.wait_ge(q_rs, S + 1)
                        dve.scalar_tensor_tensor(nmr[:, s % 4].unsqueeze(2), mv[:, s % 4, :, 0:1], -1.0,
                                                 rstd[:, s % 4].unsqueeze(2), ALU.mult, ALU.mult).then_inc(q_nmr, 1)
                    if has(tau - 9):
                        pause(dve, q_res, tau - 8, q_own)
                        dve.bn_stats(stats[:, 1, :], x_res[:, (tau - 9) % 8, :]).then_inc(q_s1, 1)
                    if has(T):
                        heads.wait()
                        at_least(dve, q_res, T)
                        heads.done(dve.scalar_tensor_tensor(headout[:].rearrange("p (h k) -> p h k", h=H), G[:, :, 0:HK],
                                                            0.0, inv[:].unsqueeze(2).broadcast_to([P, H, HK]),
                                                            ALU.max, ALU.mult))
                    if has(tau):
                        pause(dve, q_s0, tau + 1, q_own)
                        last = dve.bn_aggr(mv[:, t % 4, 0, :], stats[:, 0, :])
                    if has(tau - 9):
                        pause(dve, q_s1, tau - 8, q_own)
                        last = dve.bn_aggr(mv[:, t % 4, 1, :], stats[:, 1, :])
                    if counted(tau):
                        last.then_inc(q_mean, 1)
                    T = tau - 5
                    if has(T):
                        dve.tensor_scalar(no_edge[:], adjin[:, T % XR, :], 0.0, NEG, ALU.is_le, ALU.mult).then_inc(q_ne, 1)
                    if has(scores):
                        score.wait()
                        score.done(dve.scalar_tensor_tensor(top_l[:], top_s[:], SLOPE, top_s[:], ALU.mult, ALU.max))
                        dve.wait_ge(q_sc, scores + 1)
                        score.done(dve.scalar_tensor_tensor(leaky[:], scored[:], SLOPE, scored[:], ALU.mult, ALU.max))
                    T, r = tau - 4, (t - 4)
                    if has(T):
                        dve.wait_ge(q_xh, T + 1)
                        at_least(dve, q_sc, T - 3)
                        at_least(dve, q_diag, T - 3)
                        if isinstance(T, int) and T == 0:
                            dve.wait_ge(s_batt, 16)
                        X = bank[2 + r % 2]
                        dve.tensor_tensor(a_src[:, r % 4, :], X[:, D:D + H], batt_row[:], ALU.add).then_inc(q_asd, 1)
                        dve.tensor_copy(a_dst[:, r % 4, :], X[:, D + H:D + 2 * H]).then_inc(q_asd, 1)
                    if has(scores):
                        score.wait()
                        at_least(dve, q_e, 2 * scores)
                        dve.tensor_tensor(shifted[:], leaky[:], top_l[:].unsqueeze(2).broadcast_to([P, H, N]),
                                          ALU.subtract).then_inc(q_d, 1)
                    if splits_w1(tau):
                        part = tau - FIRST_PART
                        l, q = part // 4, part % 4
                        high, low = (w[:, l].rearrange("p c f -> p (c f)")[:, q * W1P:(q + 1) * W1P] for w in (w1_hi, w1_lo))
                        dve.wait_ge(s_whi, part + 1)
                        dve.scalar_tensor_tensor(low, raw[:, l, q * W1P:(q + 1) * W1P], g1_col[:, l, q // 2:q // 2 + 1],
                                                 high.bitcast(F32), ALU.mult, ALU.subtract).then_inc(s_wlo, 1)

                steps(dve, step)
        second = ExitStack()
        with second:
            c1_row, g2_row, beta2_row = (sb(n, [P, L, D], where=second) for n in ("c1_row", "g2_row", "beta2_row"))
            x_cur = sb("x_cur", [P, QG, TG, D], where=second)
            x_fin = sb("x_fin", [P, 2, TG, D], where=second)
            adj_raw = sb("adj_raw", [P, QG, TG, N], I32, where=second)
            mask = sb("mask", [P, QG, TG, N], where=second)
            mask_sum = sb("mask_sum", [P, TG, N], where=second)
            dots = sb("dots", [P, D], where=second)
            s_src, s_dst = (sb(n, [P, TG], where=second) for n in ("s_src", "s_dst"))
            src_b = sb("src_b", [P, TG], where=second)
            diag2 = sb("diag2", [P, TG, N], where=second)
            masked2, scored2, leaky2, shifted2 = (sb(n, [P, TG, N], where=second)
                                                  for n in ("masked2", "scored2", "leaky2", "shifted2"))
            top2, top2_s, top2_l = (sb(n, [P, TG], where=second) for n in ("top2", "top2_s", "top2_l"))
            attn = sb("attn", [P, TG, P], where=second)
            attn_T = sb("attn_T", [P, TG, P], where=second)
            row_sum, row_inv = (sb(n, [P, TG], where=second) for n in ("row_sum", "row_inv"))
            n_tok = sb("n_tok", [P, TG, D], where=second)
            nT_hi, nT_lo = (sb(n, [P, 2, KD, TOK], F32R, where=second) for n in ("nT_hi", "nT_lo"))
            base = sb("base", [P, 2, TG, D], where=second)
            hid = sb("hid", [P, RING, TOK], where=second)
            hid_hi, hid_lo = (sb(n, [P, RING, TOK], F32R, where=second) for n in ("hid_hi", "hid_lo"))
            y_tok = sb("y_tok", [P, 2, TG, D], where=second)
            st_a, st_f = (sb(n, [P, TG, 6], where=second) for n in ("st_a", "st_f"))
            mv_a, mv_f = (sb(n, [P, TG, 2], where=second) for n in ("mv_a", "mv_f"))
            ve_a, ve_f, rs_a, rs_f, nm_a, nm_f = (sb(n, [P, TG], where=second)
                                                  for n in ("ve_a", "ve_f", "rs_a", "rs_f", "nm_a", "nm_f"))

            HID, FF = (bank[0], bank[1]), (bank[2], bank[3])
            SPREAD, ATT_T = bank[4], bank[5]
            AGG = NT_B = (bank[6], bank[7])

            s_in = [sem(f"group_loaded{g}") for g in range(QG)]
            s_res = [sem(f"res_loaded{i}") for i in range(2)]
            s_out = [sem(f"group_stored{i}") for i in range(2)]
            s_own, s_own_sp, s_zero, s_scd = sem("vector_paused"), sem("sync_paused"), sem("attn_zeroed"), sem("scores_leaky")
            s_hid, s_gelu, s_split, s_ff = sem("hidden"), sem("gelu"), sem("hidden_split"), sem("ff_chunk")
            s_y = sem("ff_read")
            s_stf, s_mvf, s_rsf, s_nmf, s_yn = sem("y_stats"), sem("y_mean_var"), sem("y_rstd"), sem("y_shift"), sem("y_norm")
            s_x, s_fin = sem("x_new"), sem("out_ready")
            s_dots, s_dg = sem("dots_done"), sem("dst_diagonal")
            s_spread, s_sc, s_sh, s_at = sem("dst_spread"), sem("score_steps"), sem("shifted_ready"), sem("attn_ready")
            s_atT, s_atk, s_agg = sem("attn_T_ready"), sem("attn_T_kept"), sem("aggregated")
            s_inv, s_u, s_sta, s_mva = sem("row_sums"), sem("residual_a"), sem("a_stats"), sem("a_mean_var")
            s_rsa, s_nma, s_n = sem("a_rstd"), sem("a_shift"), sem("n_ready")
            s_nT, s_nhi, s_nlo, s_base = sem("nT"), sem("nT_hi_ready"), sem("nT_lo_ready"), sem("base_ready")
            s_b, s_g2, s_c1 = sem("bias_rows_loaded"), sem("g2_rows_loaded"), sem("c1_row_made")
            b2_row = y_tok[:, 0, 0:L, :]
            blk = second.enter_context(nc.Block())

            def slots(eng, before, some, after):
                before()
                some(0, range(1), False)
                with eng.Fori(0, LAPS - 1) as i:
                    some(i, range(1, SLOTS + 1), False)
                some(LAPS - 1, range(1, SLOTS), True)
                after((LAPS - 1) * SLOTS + SLOTS - 1)

            def layer_group(s):
                return s % SLOTS // QG, s % QG

            @blk.sync
            def _(sp):
                def load(lap, g):
                    n = lap * QG + g
                    sp.dma_start(x_cur[:, g], act_d[:, bass.ts(n, TG), :]).then_inc(s_in[g], 16)
                    sp.dma_start(adj_raw[:, g], adj_v[:, bass.ts(n, TG), :]).then_inc(s_in[g], 16)

                def load_res(lap, g):
                    n = lap * QG + g
                    sp.dma_start(x_fin[:, g % 2], res_d[:, bass.ts(n, TG), :]).then_inc(s_res[g % 2], 16)

                def before():
                    load(0, 0)
                    with nc.allow_non_contiguous_dma(reason="broadcast rows"):
                        for dst, src, done in ((c1_row[:], beta1, s_b), (b2_row, b2, s_b),
                                               (g2_row[:], g2, s_g2), (beta2_row[:], beta2, s_g2)):
                            sp.dma_start(dst.rearrange("p l d -> p (l d)"),
                                         row(src.rearrange("l d -> (l d)"), L * D)).then_inc(done, 16)
                    for g in range(1, QG):
                        load(0, g)
                    for g in range(2):
                        load_res(0, g)

                def refill(i, g, last):
                    if not last:
                        pause(sp, s_u, TG * (i * SLOTS + (L - 1) * QG + g + 1), s_own_sp)
                        load(i + 1, g)

                def put_out(i, g, last):
                    n = i * QG + g
                    pause(sp, s_fin, n + 3, s_own_sp)
                    sp.dma_start(out_v[:, bass.ts(n, TG), :], x_fin[:, g % 2]).then_inc(s_out[g % 2], 16)
                    pause(sp, s_out[g % 2], 16 * (i * (QG // 2) + g // 2 + 1), s_own_sp)
                    if g < 2:
                        load_res(i, g + 2)
                    elif not last:
                        load_res(i + 1, g - 2)

                def lap(i, last):
                    for g in range(3):
                        refill(i, g, last)
                    put_out(i, 0, last)
                    refill(i, 3, last)
                    for g in range(1, QG):
                        put_out(i, g, last)

                before()
                with sp.Fori(0, LAPS - 1) as i:
                    lap(i, False)
                lap(LAPS - 1, True)

            @blk.tensor
            def _(pe):
                pe.sem_inc(s_ff, RING)

                def spread(V, s):
                    pe.wait_ge(s_dg, V + 1)
                    pe.matmul(SPREAD[:, 0:TG * N], same_graph[:], diag2[:].rearrange("p t j -> p (t j)"),
                              start=True, stop=True).then_inc(s_spread, 1)

                def turn_attn(V, s):
                    pe.wait_ge(s_at, GPT * (V + 1))
                    for t in range(TG):
                        mm = pe.transpose(ATT_T[:, t * P:(t + 1) * P], attn[:, t, :], ident[:])
                    mm.then_inc(s_atT, 1)

                def aggregate(V, s):
                    l, g = layer_group(s)
                    pe.wait_ge(s_atk, V + 1)
                    for t in range(TG):
                        mm = pe.matmul(AGG[t // 2][:, (t % 2) * D:(t % 2 + 1) * D], attn_T[:, t, :], x_cur[:, g, t, :],
                                       start=True, stop=True)
                    mm.then_inc(s_agg, 1)

                def turn_n(V, s):
                    for k in range(KD):
                        if k == 0:
                            pe.wait_ge(s_n, TG * (V + 1))
                        for t in range(TG):
                            mm = pe.transpose(NT_B[k][:, t * P:(t + 1) * P], n_tok[:, t, k * P:(k + 1) * P], ident[:])
                        mm.then_inc(s_nT, 1)

                def hidden(U, s, c):
                    l, g = layer_group(s)
                    if c == 0:
                        pe.wait_ge(s_nlo, KD * (U + 1))
                    pe.wait_ge(s_gelu, CF * U + c + 1)
                    for k in range(KD):
                        for p, (w, a) in enumerate(((w1_hi, nT_hi), (w1_hi, nT_lo), (w1_lo, nT_hi))):
                            mm = pe.matmul(HID[c % 2][:], w[:, l, k, c * P:(c + 1) * P], a[:, s % 2, k, :],
                                           start=(k == 0 and p == 0), stop=(k == KD - 1 and p == 2))
                    mm.then_inc(s_hid, 1)

                def output(U, s, c):
                    l, g = layer_group(s)
                    pe.wait_ge(s_split, CF * U + c + 1)
                    if c == 0:
                        pe.wait_ge(s_y, TG * U + TG)
                    for t in range(TG):
                        for p, (a, w) in enumerate(((hid_hi, w2_hi), (hid_hi, w2_lo), (hid_lo, w2_hi))):
                            mm = pe.matmul(FF[t // 2][:, (t % 2) * D:(t % 2 + 1) * D], a[:, c % RING, t * P:(t + 1) * P],
                                           w[:, l, c, :], start=(c == 0 and t % 2 == 0 and p == 0),
                                           stop=(c == CF - 1 and p == 2), skip_group_check=True)
                    mm.then_inc(s_ff, 1)

                def before():
                    spread(0, 0)
                    turn_attn(0, 0)
                    aggregate(0, 0)
                    spread(1, 1)
                    turn_n(0, 0)

                def some(i, which, last):
                    for s in which:
                        U = i * SLOTS + s
                        nxt, nxt2 = not last or s + 1 < SLOTS, not last or s + 2 < SLOTS
                        for c in range(CF):
                            hidden(U, s, c)
                            if nxt and c == 0:
                                turn_attn(U + 1, s + 1)
                            if c >= 2:
                                output(U, s, c - 2)
                            if nxt and c == CF - 1:
                                turn_n(U + 1, s + 1)
                            if nxt and c == 2:
                                aggregate(U + 1, s + 1)
                            if nxt2 and c == 4:
                                spread(U + 2, s + 2)
                        output(U, s, CF - 2)
                        output(U, s, CF - 1)

                slots(pe, before, some, lambda U: None)

            @blk.scalar
            def _(act):
                act.sem_inc(s_gelu, 2)

                def gelu(U, s, c):
                    l, g = layer_group(s)
                    act.wait_ge(s_hid, CF * U + c + 1)
                    act.wait_ge(s_ff, CF * U + c + 1)
                    act.activation(hid[:, c % RING, :], HID[c % 2][:], ACT.Gelu, bias=b1_col[:, l, c:c + 1])
                    act.activation(hid_hi[:, c % RING, :], HID[c % 2][:], ACT.Gelu, bias=b1_col[:, l, c:c + 1]).then_inc(s_gelu, 1)

                def norm_y(U, par, ts):
                    for t in ts:
                        act.wait_ge(s_nmf, U + 1)
                        act.activation(y_tok[:, par, t, :], y_tok[:, par, t, :], ACT.Identity, bias=nm_f[:, t:t + 1],
                                       scale=rs_f[:, t:t + 1]).then_inc(s_yn, 1)

                def exp(V, s):
                    act.wait_ge(s_sh, V + 1)
                    at_least(act, s_atT, V)
                    for g in range(GPT):
                        act.activation(attn[g * N:(g + 1) * N, :, g * N:(g + 1) * N],
                                       shifted2[g * N:(g + 1) * N], ACT.Exp).then_inc(s_at, 1)

                def keep_attn(V, s):
                    act.wait_ge(s_atT, V + 1)
                    at_least(act, s_agg, V)
                    act.copy(attn_T[:].rearrange("p t i -> p (t i)"), ATT_T[:]).then_inc(s_atk, 1)

                def norm_n(V, s):
                    act.wait_ge(s_nma, V + 1)
                    for t in range(TG):
                        act.activation(n_tok[:, t, :], n_tok[:, t, :], ACT.Identity, bias=nm_a[:, t:t + 1],
                                       scale=rs_a[:, t:t + 1]).then_inc(s_n, 1)

                def split_n(V, s):
                    for k in range(KD):
                        act.wait_ge(s_nT, KD * V + k + 1)
                        act.copy(nT_hi[:, s % 2, k, :], NT_B[k][:]).then_inc(s_nhi, 1)

                def before():
                    act.wait_ge(s_zero, 1)
                    exp(0, 0)
                    keep_attn(0, 0)
                    norm_n(0, 0)
                    split_n(0, 0)
                    exp(1, 1)

                def some(i, which, last):
                    for s in which:
                        U = i * SLOTS + s
                        nxt, nxt2 = not last or s + 1 < SLOTS, not last or s + 2 < SLOTS
                        for c in range(CF):
                            gelu(U, s, c)
                            if nxt and c == 0:
                                keep_attn(U + 1, s + 1)
                            if s > 0 and c in (2, 3):
                                norm_y(U - 1, (s - 1) % 2, range(2 * c - 4, 2 * c - 2))
                            if nxt and c == 6:
                                norm_n(U + 1, s + 1)
                            if nxt and c == CF - 1:
                                split_n(U + 1, s + 1)
                        if nxt2:
                            exp(U + 2, s + 2)

                def after(U):
                    norm_y(U, (SLOTS - 1) % 2, range(TG))

                slots(act, before, some, after)

            @blk.gpsimd
            def _(pool):
                pool.sem_inc(s_fin, 2)
                pool.sem_inc(s_x, 4)

                def rstd_of(dst, src, wait, count, done):
                    pool.wait_ge(wait, count)
                    pool.tensor_tensor(dst[:], src[:], minus_half[:], ALU.pow).then_inc(done, 1)

                def post(i, s, nxt):
                    l, g = layer_group(s)
                    U = i * SLOTS + s
                    pool.wait_ge(s_yn, TG * (U + 1))
                    y = y_tok[:, s % 2]
                    xg = x_cur[:, g] if l < L - 1 else y
                    pool.tensor_tensor(xg, y, g2_row[:, l].unsqueeze(1).broadcast_to([P, TG, D]), ALU.mult).then_inc(s_x, 1)
                    if nxt:
                        rstd_n(U + 2)
                    pool.wait_ge(s_x, 2 * U + 5)
                    pool.tensor_tensor(xg, xg, beta2_row[:, l].unsqueeze(1).broadcast_to([P, TG, D]), ALU.add).then_inc(s_x, 1)
                    if l == L - 1:
                        pool.wait_ge(s_x, 2 * U + 6)
                        pool.wait_ge(s_res[g % 2], 16 * (i * (QG // 2) + g // 2 + 1))
                        pool.tensor_tensor(x_fin[:, g % 2], x_fin[:, g % 2], y, ALU.add).then_inc(s_fin, 1)

                def make_base(V, s):
                    l, g = layer_group(s)
                    pool.wait_ge(s_n, TG * (V + 1))
                    pool.tensor_tensor(base[:, s % 2], n_tok[:], g1_row[:, l].unsqueeze(1).broadcast_to([P, TG, D]),
                                       ALU.mult).then_inc(s_base, 1)
                    pool.wait_ge(s_base, 2 * V + 1)
                    pool.tensor_tensor(base[:, s % 2], base[:, s % 2], c1_row[:, l].unsqueeze(1).broadcast_to([P, TG, D]),
                                       ALU.add).then_inc(s_base, 1)

                def rstd_n(V):
                    rstd_of(rs_a, ve_a, s_mva, (TG + 1) * (V + 1), s_rsa)

                def rstd_y(U):
                    rstd_of(rs_f, ve_f, s_mvf, (TG + 1) * (U + 1), s_rsf)

                def before():
                    pool.wait_ge(s_b, 32)
                    pool.tensor_tensor(c1_row[:], c1_row[:], b2_row, ALU.add).then_inc(s_c1, 1)
                    rstd_n(0)
                    pool.wait_ge(s_c1, 1)
                    make_base(0, 0)
                    pool.wait_ge(s_g2, 32)

                def some(i, which, last):
                    for s in which:
                        U, nxt = i * SLOTS + s, not last or s + 1 < SLOTS
                        if s > 0:
                            rstd_y(U - 1)
                            post(i, s - 1, nxt)
                        elif nxt:
                            rstd_n(U + 1)
                        if nxt:
                            make_base(U + 1, s + 1)

                def after(U):
                    rstd_y(U)
                    post(LAPS - 1, SLOTS - 1, False)

                slots(pool, before, some, after)

            @blk.vector
            def _(dve):
                dve.memset(attn[:], 0.0).then_inc(s_zero, 1)
                dve.sem_inc(s_y, TG)
                score = Steps(dve, s_sc, 7)

                def split(U, c):
                    dve.wait_ge(s_gelu, CF * U + c + 3)
                    dve.tensor_tensor(hid_lo[:, c % RING, :], hid[:, c % RING, :], hid_hi[:, c % RING, :].bitcast(F32),
                                      ALU.subtract).then_inc(s_split, 1)

                def take_y(i, s):
                    U = i * SLOTS + s
                    dve.wait_ge(s_ff, CF * (U + 1) + RING)
                    dve.wait_ge(s_base, 2 * U + 2)
                    dve.wait_ge(s_x, 2 * U + 2)
                    if 0 <= s - 2 - (L - 1) * QG:
                        dve.wait_ge(s_fin, i * QG + s + 1 - (L - 1) * QG)
                    elif s < 2:
                        dve.wait_ge(s_fin, i * QG + s + 1)
                    for t in range(TG):
                        dve.tensor_tensor(y_tok[:, s % 2, t, :], FF[t // 2][:, (t % 2) * D:(t % 2 + 1) * D], base[:, s % 2, t, :],
                                          ALU.add).then_inc(s_y, 1)

                def stats_y(U, s):
                    for t in range(TG):
                        dve.wait_ge(s_y, TG * (U + 1) + t + 1)
                        dve.bn_stats(st_f[:, t, :], y_tok[:, s % 2, t, :]).then_inc(s_stf, 1)
                    pause(dve, s_stf, TG * U + TG, s_own)
                    for t in range(TG):
                        dve.bn_aggr(mv_f[:, t, :], st_f[:, t, :]).then_inc(s_mvf, 1)
                    dve.wait_ge(s_mvf, (TG + 1) * U + TG)
                    dve.tensor_scalar(ve_f[:].unsqueeze(2), mv_f[:, :, 1:2], EPS, None, ALU.add).then_inc(s_mvf, 1)

                def shift_y(U, s):
                    dve.wait_ge(s_rsf, U + 1)
                    dve.scalar_tensor_tensor(nm_f[:].unsqueeze(2), mv_f[:, :, 0:1], -1.0, rs_f[:].unsqueeze(2),
                                             ALU.mult, ALU.mult).then_inc(s_nmf, 1)

                def dots_of(i, s, ts):
                    l, g = layer_group(s)
                    V = i * SLOTS + s
                    if ts[0] == 0:
                        if l == 0:
                            dve.wait_ge(s_in[g], 32 * (i + s // SLOTS + 1))
                        else:
                            dve.wait_ge(s_x, 2 * (V - QG) + 6)
                    for t in ts:
                        for j, dst in enumerate((s_src, s_dst)):
                            n = 2 * t + j
                            at_least(dve, s_dots, 8 * V + n)
                            dve.tensor_tensor_reduce(dots[:], x_cur[:, g, t, :], att_row[:, l, j, :], 1.0, 0.0,
                                                     ALU.mult, ALU.add, dst[:, t:t + 1]).then_inc(s_dots, 1)

                def diagonal(i, s):
                    l, g = layer_group(s)
                    V = i * SLOTS + s
                    dve.wait_ge(s_dots, 2 * TG * (V + 1))
                    at_least(dve, s_spread, V)
                    dve.tensor_tensor(diag2[:], node_of[:].unsqueeze(1).broadcast_to([P, TG, N]),
                                      s_dst[:].unsqueeze(2).broadcast_to([P, TG, N]), ALU.mult).then_inc(s_dg, 1)
                    score.unit(V)
                    score.done(dve.tensor_scalar(src_b[:], s_src[:], attb_row[:, l:l + 1], None, ALU.add))
                    if l == 0:
                        score.done(dve.tensor_tensor(mask_sum[:], adj_raw[:, g], node_of[:].unsqueeze(1).broadcast_to([P, TG, N]),
                                                     ALU.add))
                        score.wait()
                        score.done(dve.tensor_scalar(mask[:, g], mask_sum[:], 0.0, NEG, ALU.is_le, ALU.mult))
                        score.wait()
                    else:
                        score.k += 2
                        dve.sem_inc(s_sc, 2)

                def scores(i, s):
                    l, g = layer_group(s)
                    V = i * SLOTS + s
                    score.wait()
                    dve.wait_ge(s_spread, V + 1)
                    score.done(dve.tensor_tensor(masked2[:], SPREAD[:, 0:TG * N].rearrange("p (t j) -> p t j", t=TG), mask[:, g],
                                                 ALU.add))
                    score.wait()
                    score.done(dve.tensor_reduce(top2[:], masked2[:], AX, ALU.max))
                    dve.tensor_tensor(scored2[:], masked2[:], src_b[:].unsqueeze(2).broadcast_to([P, TG, N]),
                                      ALU.add).then_inc(s_scd, 1)
                    score.wait()
                    score.done(dve.tensor_tensor(top2_s[:], top2[:], src_b[:], ALU.add))
                    dve.wait_ge(s_scd, 2 * V + 1)
                    dve.scalar_tensor_tensor(leaky2[:], scored2[:], SLOPE, scored2[:], ALU.mult, ALU.max).then_inc(s_scd, 1)
                    score.wait()
                    score.done(dve.scalar_tensor_tensor(top2_l[:], top2_s[:], SLOPE, top2_s[:], ALU.mult, ALU.max))
                    score.wait()
                    dve.wait_ge(s_scd, 2 * V + 2)
                    at_least(dve, s_at, GPT * V)
                    dve.tensor_tensor(shifted2[:], leaky2[:], top2_l[:].unsqueeze(2).broadcast_to([P, TG, N]),
                                      ALU.subtract).then_inc(s_sh, 1)

                def sums(V):
                    dve.wait_ge(s_at, GPT * (V + 1))
                    dve.tensor_reduce(row_sum[:], attn[:], AX, ALU.add).then_inc(s_inv, 1)
                    dve.wait_ge(s_inv, 2 * V + 1)
                    dve.reciprocal(row_inv[:], row_sum[:]).then_inc(s_inv, 1)

                def residual(i, s):
                    l, g = layer_group(s)
                    V = i * SLOTS + s
                    dve.wait_ge(s_agg, V + 1)
                    dve.wait_ge(s_inv, 2 * V + 2)
                    at_least(dve, s_nT, KD * V)
                    at_least(dve, s_base, 2 * V - 1)
                    for t in range(TG):
                        dve.scalar_tensor_tensor(n_tok[:, t, :], AGG[t // 2][:, (t % 2) * D:(t % 2 + 1) * D], row_inv[:, t:t + 1],
                                                 x_cur[:, g, t, :], ALU.mult, ALU.add).then_inc(s_u, 1)

                def stats_n(V):
                    for t in range(TG):
                        dve.wait_ge(s_u, TG * V + t + 1)
                        dve.bn_stats(st_a[:, t, :], n_tok[:, t, :]).then_inc(s_sta, 1)
                    pause(dve, s_sta, TG * V + TG, s_own)
                    for t in range(TG):
                        dve.bn_aggr(mv_a[:, t, :], st_a[:, t, :]).then_inc(s_mva, 1)
                    dve.wait_ge(s_mva, (TG + 1) * V + TG)
                    dve.tensor_scalar(ve_a[:].unsqueeze(2), mv_a[:, :, 1:2], EPS, None, ALU.add).then_inc(s_mva, 1)

                def shift_n(V):
                    dve.wait_ge(s_rsa, V + 1)
                    dve.scalar_tensor_tensor(nm_a[:].unsqueeze(2), mv_a[:, :, 0:1], -1.0, rs_a[:].unsqueeze(2),
                                             ALU.mult, ALU.mult).then_inc(s_nma, 1)

                def split_n(V, s):
                    for k in range(KD):
                        dve.wait_ge(s_nhi, KD * V + k + 1)
                        dve.tensor_tensor(nT_lo[:, s % 2, k, :], NT_B[k][:], nT_hi[:, s % 2, k, :].bitcast(F32),
                                          ALU.subtract).then_inc(s_nlo, 1)

                def before():
                    for V in range(2):
                        dots_of(0, V, range(TG))
                        diagonal(0, V)
                        scores(0, V)
                        if V == 0:
                            sums(0)
                            residual(0, 0)
                            stats_n(0)
                            shift_n(0)
                    split_n(0, 0)

                def some(i, which, last):
                    for s in which:
                        U = i * SLOTS + s
                        nxt, nxt2 = not last or s + 1 < SLOTS, not last or s + 2 < SLOTS
                        if s > 0:
                            take_y(i, s - 1)
                        if nxt2:
                            dots_of(i, s + 2, range(0, 2))
                        split(U, 0)
                        if s > 0:
                            stats_y(U - 1, s - 1)
                        split(U, 1)
                        if s > 0:
                            shift_y(U - 1, s - 1)
                        if nxt2:
                            dots_of(i, s + 2, range(2, 4))
                            diagonal(i, s + 2)
                        split(U, 2)
                        if nxt:
                            sums(U + 1)
                            residual(i, s + 1)
                        split(U, 3)
                        if nxt:
                            stats_n(U + 1)
                        split(U, 4)
                        if nxt:
                            shift_n(U + 1)
                        if nxt2:
                            scores(i, s + 2)
                        split(U, 5)
                        split(U, 6)
                        split(U, 7)
                        if nxt:
                            split_n(U + 1, s + 1)

                def after(U):
                    take_y(LAPS - 1, SLOTS - 1)
                    stats_y(U, SLOTS - 1)
                    shift_y(U, SLOTS - 1)

                slots(dve, before, some, after)

_INS = ['x', 'adj', 'L0_gnn_W_proj', 'L0_gnn_W_att', 'L0_gnn_b_att', 'L1_gnn_attn_w', 'L1_gnn_attn_b', 'L1_gnn_W1',
        'L1_gnn_b1', 'L1_gnn_W2', 'L1_gnn_b2', 'L1_gnn_g1', 'L1_gnn_beta1', 'L1_gnn_g2', 'L1_gnn_beta2']
_OUTS = [((128, 64, 256), 'float32')]


def kernel(**inputs):
    import numpy as _np
    import concourse.bacc as _bacc
    from concourse import mybir as _mybir
    from concourse.bass_utils import run_bass_kernel_spmd as _run

    nc = _bacc.Bacc("TRN2", target_bir_lowering=False, num_devices=1)
    arrays, args = {}, []
    for name in _INS:
        a = _np.ascontiguousarray(inputs[name])
        arrays[f"in_{name}_dram"] = a
        args.append(nc.dram_tensor(f"in_{name}_dram", a.shape, _mybir.dt.from_np(a.dtype), kind="ExternalInput").ap())
    for i, (shape, dtype) in enumerate(_OUTS):
        dt = _mybir.dt.from_np(_np.dtype(dtype))
        args.append(nc.dram_tensor(f"out_{i}_dram", shape, dt, kind="ExternalOutput").ap())
    graph_net(nc, *args)
    r = _run(nc, [arrays], core_ids=[0])
    got = tuple(r.results[0][f"out_{i}_dram"] for i in range(len(_OUTS)))
    return got[0]
```
